# Optimizing a Trainium2 kernel written in Bass

```python
import numpy as np
import jax
import jax.numpy as jnp

def _softmax(x, axis=-1):
    return jax.nn.softmax(x, axis=axis)

def _gelu(x):
    return jax.nn.gelu(x, approximate=True)

def _silu(x):
    return jax.nn.silu(x)

def _sigmoid(x):
    return jax.nn.sigmoid(x)

def _layernorm(x, axis=-1, eps=1e-05):
    m = jnp.mean(x, axis=axis, keepdims=True)
    v = jnp.var(x, axis=axis, keepdims=True)
    return (x - m) / jnp.sqrt(v + eps)

def _scatter_add(tgt, idx, src, axis=0):
    return tgt.at[idx].add(src)

def _segment_sum(src, seg, n):
    return jax.ops.segment_sum(src, seg, n)
kernel_name = 'mk_xattn_seq_d2_seqx_r8_a694d0'

def setup_inputs(seed: int=0):
    np.random.seed(seed)
    _w = jnp.asarray

    def _rec_inputs():
        import jax
        import jax.numpy as jnp
        _rk = jax.random.key(seed)
        x = -0.0002928 + 1 * jax.random.normal(jax.random.fold_in(_rk, 1), (16, 256, 128), jnp.float32)
        _lenS = 256 - jax.random.randint(jax.random.fold_in(_rk, 7), (16,), 0, max(1, 256 // 4) + 1, jnp.int32)
        _lenS2 = 1601 - jax.random.randint(jax.random.fold_in(_rk, 8), (16,), 0, max(1, 1601 // 4) + 1, jnp.int32)
        _ctx_1024P = jax.random.normal(jax.random.fold_in(_rk, 11), (16, 16, 128), jnp.float32)
        _ctx_1024c = jax.random.dirichlet(jax.random.fold_in(_rk, 511), 0.3 * jnp.ones((16,), jnp.float32), (16, 1601))
        _ctx_1024t = jnp.einsum('bsk,bkd->bsd', _ctx_1024c, _ctx_1024P)
        _ctx_1024t = _ctx_1024t * jax.lax.rsqrt(jnp.mean(jnp.square(_ctx_1024t)) + 1e-12) * 0.953939
        ctx_1024 = -1.39393e-06 + 0.999914 * (_ctx_1024t + 0.3 * jax.random.normal(jax.random.fold_in(_rk, 611), (16, 1601, 128), jnp.float32))
        _validS = jnp.arange(256)[None, :] < _lenS[:, None]
        _validS2 = jnp.arange(1601)[None, :] < _lenS2[:, None]
        _causal = jnp.tril(jnp.ones((256, 256), dtype=bool))
        mask_BxSxS_ik0 = jnp.where(jnp.broadcast_to(_validS[:, None, :], (16, 256, 256)), 0, 1).astype(jnp.int32)
        mask_BxSxS2_if1 = jnp.where(jnp.ones((16, 256, 1601), dtype=bool), 1, 0).astype(jnp.int32)
        return (x, ctx_1024, mask_BxSxS_ik0, mask_BxSxS2_if1)
    x, ctx_1024, mask_BxSxS_ik0, mask_BxSxS2_if1 = _rec_inputs()

    def _L0_xattn_setup():
        import jax, jax.numpy as jnp
        import numpy as np
        B, S, SE, D, H, FF, E, K = (2, 256, 256, 128, 16, 512, 8, 2)
        HD = D // H

        def _layernorm(x, g, b):
            m = x.mean(-1, keepdims=True)
            v = ((x - m) ** 2).mean(-1, keepdims=True)
            return (x - m) / jnp.sqrt(v + 1e-05) * g + b

        def _attn(q_in, k_in, v_in, wq, bq, wk, bk, wv, bv, wo, bo, causal):
            Bq, Sq, Dm = q_in.shape
            Sk = k_in.shape[1]
            Q = (q_in @ wq + bq).reshape(Bq, Sq, H, HD)
            Kp = (k_in @ wk + bk).reshape(Bq, Sk, H, HD)
            V = (v_in @ wv + bv).reshape(Bq, Sk, H, HD)
            scores = jnp.einsum('bqhd,bkhd->bhqk', Q, Kp) / jnp.sqrt(jnp.float32(HD))
            if causal:
                mask = jnp.tril(jnp.ones((Sq, Sk), bool))
                scores = jnp.where(mask, scores, -jnp.inf)
            a = jax.nn.softmax(scores, axis=-1)
            o = jnp.einsum('bhqk,bkhd->bqhd', a, V).reshape(Bq, Sq, Dm)
            return o @ wo + bo

        def _moe(x, rw, rb, w1, b1, w2, b2):
            T = x.shape[0] * x.shape[1]
            xf = x.reshape(T, D)
            router_weights = jax.nn.softmax(xf @ rw + rb, axis=-1)
            topw, topi = jax.lax.top_k(router_weights, K)
            topw = jax.nn.softmax(topw, axis=-1)
            combine = jnp.zeros((T, E), xf.dtype).at[jnp.arange(T)[:, None], topi].add(topw)
            h = jax.nn.gelu(jnp.einsum('td,edf->etf', xf, w1) + b1[:, None, :], approximate=False)
            eo = jnp.einsum('etf,efd->etd', h, w2) + b2[:, None, :]
            out = jnp.einsum('etd,te->td', eo, combine)
            return out.reshape(x.shape)
        key = jax.random.key(seed)
        ks = jax.random.split(key, 32)
        w = lambda k, shape: jax.random.normal(k, shape, jnp.float32) * 0.02
        inp = {'x': jax.random.normal(ks[0], (B, S, D), jnp.float32), 'encoder_output': jax.random.normal(ks[1], (B, SE, D), jnp.float32), 'sa_wq': w(ks[2], (D, D)), 'sa_bq': jnp.zeros((D,), jnp.float32), 'sa_wk': w(ks[3], (D, D)), 'sa_bk': jnp.zeros((D,), jnp.float32), 'sa_wv': w(ks[4], (D, D)), 'sa_bv': jnp.zeros((D,), jnp.float32), 'sa_wo': w(ks[5], (D, D)), 'sa_bo': jnp.zeros((D,), jnp.float32), 'ca_wq': w(ks[6], (D, D)), 'ca_bq': jnp.zeros((D,), jnp.float32), 'ca_wk': w(ks[7], (D, D)), 'ca_bk': jnp.zeros((D,), jnp.float32), 'ca_wv': w(ks[8], (D, D)), 'ca_bv': jnp.zeros((D,), jnp.float32), 'ca_wo': w(ks[9], (D, D)), 'ca_bo': jnp.zeros((D,), jnp.float32), 'ln1_g': jnp.ones((D,), jnp.float32), 'ln1_b': jnp.zeros((D,), jnp.float32), 'ln2_g': jnp.ones((D,), jnp.float32), 'ln2_b': jnp.zeros((D,), jnp.float32), 'ln3_g': jnp.ones((D,), jnp.float32), 'ln3_b': jnp.zeros((D,), jnp.float32), 'router_w': w(ks[10], (D, E)), 'router_b': jnp.zeros((E,), jnp.float32), 'e_w1': w(ks[11], (E, D, FF)), 'e_b1': jnp.zeros((E, FF), jnp.float32), 'e_w2': w(ks[12], (E, FF, D)), 'e_b2': jnp.zeros((E, D), jnp.float32)}
        return inp
    _L0_xattn_all = _L0_xattn_setup()
    _L0_xattn_in = {k: v for k, v in _L0_xattn_all.items() if k in ('sa_wq', 'sa_bq', 'sa_wk', 'sa_bk', 'sa_wv', 'sa_bv', 'sa_wo', 'sa_bo', 'ca_wq', 'ca_bq', 'ca_wk', 'ca_bk', 'ca_wv', 'ca_bv', 'ca_wo', 'ca_bo', 'ln1_g', 'ln1_b', 'ln2_g', 'ln2_b', 'ln3_g', 'ln3_b', 'router_w', 'router_b', 'e_w1', 'e_b1', 'e_w2', 'e_b2')}
    del _L0_xattn_all

    def _L1_xattn_setup():
        import jax, jax.numpy as jnp
        import numpy as np
        B, T, S_ENC, D, H, E, K = (4, 128, 64, 128, 16, 8, 2)
        DK = D // H
        HID = 4 * D
        NEG = -65504.0
        EPS = 1e-05

        def rmsnorm(x, w):
            return w * (x * jax.lax.rsqrt(jnp.mean(x * x, axis=-1, keepdims=True) + EPS))

        def mha(xq, xk, xv, mask, wq, wk, wv, wo):
            q = jnp.einsum('bsd,ed->bse', xq, wq).reshape(xq.shape[0], -1, H, DK).transpose(0, 2, 1, 3)
            k = jnp.einsum('bsd,ed->bse', xk, wk).reshape(xk.shape[0], -1, H, DK).transpose(0, 2, 1, 3)
            v = jnp.einsum('bsd,ed->bse', xv, wv).reshape(xv.shape[0], -1, H, DK).transpose(0, 2, 1, 3)
            scores = jnp.einsum('bhqd,bhkd->bhqk', q, k) / jnp.sqrt(jnp.float32(DK))
            scores = jnp.where(mask[:, None, :, :] == 0, NEG, scores)
            attn = jax.nn.softmax(scores, axis=-1)
            out = jnp.einsum('bhqk,bhkd->bhqd', attn, v)
            out = out.transpose(0, 2, 1, 3).reshape(xq.shape[0], -1, D)
            return jnp.einsum('bsd,ed->bse', out, wo)

        def moe_ffn(x, gate_w, exp_w1, exp_w2, sh_w1, sh_w2):
            b, s, d = x.shape
            xf = x.reshape(-1, d)
            sh = jnp.einsum('nd,hd->nh', xf, sh_w1)
            sh = jax.nn.silu(sh)
            sh = jnp.einsum('nh,dh->nd', sh, sh_w2)
            logits = jnp.einsum('nd,ed->ne', xf, gate_w)
            topk_vals, topk_idx = jax.lax.top_k(logits, K)
            topk_gates = jax.nn.softmax(topk_vals, axis=-1)
            n = xf.shape[0]
            gates = jnp.zeros((n, E), dtype=xf.dtype).at[jnp.arange(n)[:, None], topk_idx].set(topk_gates)
            h = jnp.einsum('nd,ehd->neh', xf, exp_w1)
            h = jax.nn.silu(h)
            eo = jnp.einsum('neh,edh->ned', h, exp_w2)
            sel = jnp.einsum('ned,ne->nd', eo, gates)
            return (sh + sel).reshape(b, s, d)
        key = jax.random.key(seed)
        ks = jax.random.split(key, 16)
        sd = 1.0 / np.sqrt(D)
        inp = {'x': jax.random.normal(ks[0], (B, T, D), jnp.float32), 'encoder_output': jax.random.normal(ks[1], (B, S_ENC, D), jnp.float32), 'tgt_mask': jnp.tril(jnp.ones((T, T), jnp.int32))[None].repeat(B, 0), 'src_mask': jnp.ones((B, T, S_ENC), jnp.int32), 'norm1_w': jnp.ones((D,), jnp.float32), 'norm2_w': jnp.ones((D,), jnp.float32), 'norm3_w': jnp.ones((D,), jnp.float32), 'sa_wq': jax.random.normal(ks[2], (D, D), jnp.float32) * sd, 'sa_wk': jax.random.normal(ks[3], (D, D), jnp.float32) * sd, 'sa_wv': jax.random.normal(ks[4], (D, D), jnp.float32) * sd, 'sa_wo': jax.random.normal(ks[5], (D, D), jnp.float32) * sd, 'ca_wq': jax.random.normal(ks[6], (D, D), jnp.float32) * sd, 'ca_wk': jax.random.normal(ks[7], (D, D), jnp.float32) * sd, 'ca_wv': jax.random.normal(ks[8], (D, D), jnp.float32) * sd, 'ca_wo': jax.random.normal(ks[9], (D, D), jnp.float32) * sd, 'gate_w': jax.random.normal(ks[10], (E, D), jnp.float32) * 0.02, 'exp_w1': jax.random.normal(ks[11], (E, HID, D), jnp.float32) * sd, 'exp_w2': jax.random.normal(ks[12], (E, D, HID), jnp.float32) / np.sqrt(HID), 'sh_w1': jax.random.normal(ks[13], (HID, D), jnp.float32) * sd, 'sh_w2': jax.random.normal(ks[14], (D, HID), jnp.float32) / np.sqrt(HID)}
        return inp
    _L1_xattn_all = _L1_xattn_setup()
    _L1_xattn_in = {k: v for k, v in _L1_xattn_all.items() if k in ('norm1_w', 'norm2_w', 'norm3_w', 'sa_wq', 'sa_wk', 'sa_wv', 'sa_wo', 'ca_wq', 'ca_wk', 'ca_wv', 'ca_wo', 'gate_w', 'exp_w1', 'exp_w2', 'sh_w1', 'sh_w2')}
    del _L1_xattn_all
    return {'x': x, 'ctx_1024': ctx_1024, 'mask_BxSxS_ik0': mask_BxSxS_ik0, 'mask_BxSxS2_if1': mask_BxSxS2_if1, 'L0_xattn_sa_wq': _L0_xattn_in['sa_wq'], 'L0_xattn_sa_bq': _L0_xattn_in['sa_bq'], 'L0_xattn_sa_wk': _L0_xattn_in['sa_wk'], 'L0_xattn_sa_bk': _L0_xattn_in['sa_bk'], 'L0_xattn_sa_wv': _L0_xattn_in['sa_wv'], 'L0_xattn_sa_bv': _L0_xattn_in['sa_bv'], 'L0_xattn_sa_wo': _L0_xattn_in['sa_wo'], 'L0_xattn_sa_bo': _L0_xattn_in['sa_bo'], 'L0_xattn_ca_wq': _L0_xattn_in['ca_wq'], 'L0_xattn_ca_bq': _L0_xattn_in['ca_bq'], 'L0_xattn_ca_wk': _L0_xattn_in['ca_wk'], 'L0_xattn_ca_bk': _L0_xattn_in['ca_bk'], 'L0_xattn_ca_wv': _L0_xattn_in['ca_wv'], 'L0_xattn_ca_bv': _L0_xattn_in['ca_bv'], 'L0_xattn_ca_wo': _L0_xattn_in['ca_wo'], 'L0_xattn_ca_bo': _L0_xattn_in['ca_bo'], 'L0_xattn_ln1_g': _L0_xattn_in['ln1_g'], 'L0_xattn_ln1_b': _L0_xattn_in['ln1_b'], 'L0_xattn_ln2_g': _L0_xattn_in['ln2_g'], 'L0_xattn_ln2_b': _L0_xattn_in['ln2_b'], 'L0_xattn_ln3_g': _L0_xattn_in['ln3_g'], 'L0_xattn_ln3_b': _L0_xattn_in['ln3_b'], 'L0_xattn_router_w': _L0_xattn_in['router_w'], 'L0_xattn_router_b': _L0_xattn_in['router_b'], 'L0_xattn_e_w1': _L0_xattn_in['e_w1'], 'L0_xattn_e_b1': _L0_xattn_in['e_b1'], 'L0_xattn_e_w2': _L0_xattn_in['e_w2'], 'L0_xattn_e_b2': _L0_xattn_in['e_b2'], 'L1_xattn_norm1_w': _L1_xattn_in['norm1_w'], 'L1_xattn_norm2_w': _L1_xattn_in['norm2_w'], 'L1_xattn_norm3_w': _L1_xattn_in['norm3_w'], 'L1_xattn_sa_wq': _L1_xattn_in['sa_wq'], 'L1_xattn_sa_wk': _L1_xattn_in['sa_wk'], 'L1_xattn_sa_wv': _L1_xattn_in['sa_wv'], 'L1_xattn_sa_wo': _L1_xattn_in['sa_wo'], 'L1_xattn_ca_wq': _L1_xattn_in['ca_wq'], 'L1_xattn_ca_wk': _L1_xattn_in['ca_wk'], 'L1_xattn_ca_wv': _L1_xattn_in['ca_wv'], 'L1_xattn_ca_wo': _L1_xattn_in['ca_wo'], 'L1_xattn_gate_w': _L1_xattn_in['gate_w'], 'L1_xattn_exp_w1': _L1_xattn_in['exp_w1'], 'L1_xattn_exp_w2': _L1_xattn_in['exp_w2'], 'L1_xattn_sh_w1': _L1_xattn_in['sh_w1'], 'L1_xattn_sh_w2': _L1_xattn_in['sh_w2']}

def reference(x, ctx_1024, mask_BxSxS_ik0, mask_BxSxS2_if1, L0_xattn_sa_wq, L0_xattn_sa_bq, L0_xattn_sa_wk, L0_xattn_sa_bk, L0_xattn_sa_wv, L0_xattn_sa_bv, L0_xattn_sa_wo, L0_xattn_sa_bo, L0_xattn_ca_wq, L0_xattn_ca_bq, L0_xattn_ca_wk, L0_xattn_ca_bk, L0_xattn_ca_wv, L0_xattn_ca_bv, L0_xattn_ca_wo, L0_xattn_ca_bo, L0_xattn_ln1_g, L0_xattn_ln1_b, L0_xattn_ln2_g, L0_xattn_ln2_b, L0_xattn_ln3_g, L0_xattn_ln3_b, L0_xattn_router_w, L0_xattn_router_b, L0_xattn_e_w1, L0_xattn_e_b1, L0_xattn_e_w2, L0_xattn_e_b2, L1_xattn_norm1_w, L1_xattn_norm2_w, L1_xattn_norm3_w, L1_xattn_sa_wq, L1_xattn_sa_wk, L1_xattn_sa_wv, L1_xattn_sa_wo, L1_xattn_ca_wq, L1_xattn_ca_wk, L1_xattn_ca_wv, L1_xattn_ca_wo, L1_xattn_gate_w, L1_xattn_exp_w1, L1_xattn_exp_w2, L1_xattn_sh_w1, L1_xattn_sh_w2):
    import jax
    import jax.numpy as jnp

    def _L0_xattn_ref(x, encoder_output, sa_wq, sa_bq, sa_wk, sa_bk, sa_wv, sa_bv, sa_wo, sa_bo, ca_wq, ca_bq, ca_wk, ca_bk, ca_wv, ca_bv, ca_wo, ca_bo, ln1_g, ln1_b, ln2_g, ln2_b, ln3_g, ln3_b, router_w, router_b, e_w1, e_b1, e_w2, e_b2):
        import jax, jax.numpy as jnp
        import numpy as np
        B, S, SE, D, H, FF, E, K = (2, 256, 256, 128, 16, 512, 8, 2)
        HD = D // H

        def _layernorm(x, g, b):
            m = x.mean(-1, keepdims=True)
            v = ((x - m) ** 2).mean(-1, keepdims=True)
            return (x - m) / jnp.sqrt(v + 1e-05) * g + b

        def _attn(q_in, k_in, v_in, wq, bq, wk, bk, wv, bv, wo, bo, causal):
            Bq, Sq, Dm = q_in.shape
            Sk = k_in.shape[1]
            Q = (q_in @ wq + bq).reshape(Bq, Sq, H, HD)
            Kp = (k_in @ wk + bk).reshape(Bq, Sk, H, HD)
            V = (v_in @ wv + bv).reshape(Bq, Sk, H, HD)
            scores = jnp.einsum('bqhd,bkhd->bhqk', Q, Kp) / jnp.sqrt(jnp.float32(HD))
            if causal:
                mask = jnp.tril(jnp.ones((Sq, Sk), bool))
                scores = jnp.where(mask, scores, -jnp.inf)
            a = jax.nn.softmax(scores, axis=-1)
            o = jnp.einsum('bhqk,bkhd->bqhd', a, V).reshape(Bq, Sq, Dm)
            return o @ wo + bo

        def _moe(x, rw, rb, w1, b1, w2, b2):
            T = x.shape[0] * x.shape[1]
            xf = x.reshape(T, D)
            router_weights = jax.nn.softmax(xf @ rw + rb, axis=-1)
            topw, topi = jax.lax.top_k(router_weights, K)
            topw = jax.nn.softmax(topw, axis=-1)
            combine = jnp.zeros((T, E), xf.dtype).at[jnp.arange(T)[:, None], topi].add(topw)
            h = jax.nn.gelu(jnp.einsum('td,edf->etf', xf, w1) + b1[:, None, :], approximate=False)
            eo = jnp.einsum('etf,efd->etd', h, w2) + b2[:, None, :]
            out = jnp.einsum('etd,te->td', eo, combine)
            return out.reshape(x.shape)
        x = _layernorm(x + _attn(x, x, x, sa_wq, sa_bq, sa_wk, sa_bk, sa_wv, sa_bv, sa_wo, sa_bo, True), ln1_g, ln1_b)
        x = _layernorm(x + _attn(x, encoder_output, encoder_output, ca_wq, ca_bq, ca_wk, ca_bk, ca_wv, ca_bv, ca_wo, ca_bo, False), ln2_g, ln2_b)
        x = _layernorm(x + _moe(x, router_w, router_b, e_w1, e_b1, e_w2, e_b2), ln3_g, ln3_b)
        return x

    def _L1_xattn_ref(x, encoder_output, tgt_mask, src_mask, norm1_w, norm2_w, norm3_w, sa_wq, sa_wk, sa_wv, sa_wo, ca_wq, ca_wk, ca_wv, ca_wo, gate_w, exp_w1, exp_w2, sh_w1, sh_w2):
        import jax, jax.numpy as jnp
        import numpy as np
        B, T, S_ENC, D, H, E, K = (4, 128, 64, 128, 16, 8, 2)
        DK = D // H
        HID = 4 * D
        NEG = -65504.0
        EPS = 1e-05

        def rmsnorm(x, w):
            return w * (x * jax.lax.rsqrt(jnp.mean(x * x, axis=-1, keepdims=True) + EPS))

        def mha(xq, xk, xv, mask, wq, wk, wv, wo):
            q = jnp.einsum('bsd,ed->bse', xq, wq).reshape(xq.shape[0], -1, H, DK).transpose(0, 2, 1, 3)
            k = jnp.einsum('bsd,ed->bse', xk, wk).reshape(xk.shape[0], -1, H, DK).transpose(0, 2, 1, 3)
            v = jnp.einsum('bsd,ed->bse', xv, wv).reshape(xv.shape[0], -1, H, DK).transpose(0, 2, 1, 3)
            scores = jnp.einsum('bhqd,bhkd->bhqk', q, k) / jnp.sqrt(jnp.float32(DK))
            scores = jnp.where(mask[:, None, :, :] == 0, NEG, scores)
            attn = jax.nn.softmax(scores, axis=-1)
            out = jnp.einsum('bhqk,bhkd->bhqd', attn, v)
            out = out.transpose(0, 2, 1, 3).reshape(xq.shape[0], -1, D)
            return jnp.einsum('bsd,ed->bse', out, wo)

        def moe_ffn(x, gate_w, exp_w1, exp_w2, sh_w1, sh_w2):
            b, s, d = x.shape
            xf = x.reshape(-1, d)
            sh = jnp.einsum('nd,hd->nh', xf, sh_w1)
            sh = jax.nn.silu(sh)
            sh = jnp.einsum('nh,dh->nd', sh, sh_w2)
            logits = jnp.einsum('nd,ed->ne', xf, gate_w)
            topk_vals, topk_idx = jax.lax.top_k(logits, K)
            topk_gates = jax.nn.softmax(topk_vals, axis=-1)
            n = xf.shape[0]
            gates = jnp.zeros((n, E), dtype=xf.dtype).at[jnp.arange(n)[:, None], topk_idx].set(topk_gates)
            h = jnp.einsum('nd,ehd->neh', xf, exp_w1)
            h = jax.nn.silu(h)
            eo = jnp.einsum('neh,edh->ned', h, exp_w2)
            sel = jnp.einsum('ned,ne->nd', eo, gates)
            return (sh + sel).reshape(b, s, d)
        xn = rmsnorm(x, norm1_w)
        h = x + mha(xn, xn, xn, tgt_mask, sa_wq, sa_wk, sa_wv, sa_wo)
        hn = rmsnorm(h, norm2_w)
        h = h + mha(hn, encoder_output, encoder_output, src_mask, ca_wq, ca_wk, ca_wv, ca_wo)
        hn = rmsnorm(h, norm3_w)
        return h + moe_ffn(hn, gate_w, exp_w1, exp_w2, sh_w1, sh_w2)
    x = _L0_xattn_ref(x, ctx_1024, L0_xattn_sa_wq, L0_xattn_sa_bq, L0_xattn_sa_wk, L0_xattn_sa_bk, L0_xattn_sa_wv, L0_xattn_sa_bv, L0_xattn_sa_wo, L0_xattn_sa_bo, L0_xattn_ca_wq, L0_xattn_ca_bq, L0_xattn_ca_wk, L0_xattn_ca_bk, L0_xattn_ca_wv, L0_xattn_ca_bv, L0_xattn_ca_wo, L0_xattn_ca_bo, L0_xattn_ln1_g, L0_xattn_ln1_b, L0_xattn_ln2_g, L0_xattn_ln2_b, L0_xattn_ln3_g, L0_xattn_ln3_b, L0_xattn_router_w, L0_xattn_router_b, L0_xattn_e_w1, L0_xattn_e_b1, L0_xattn_e_w2, L0_xattn_e_b2)
    x = _L1_xattn_ref(x, ctx_1024, mask_BxSxS_ik0, mask_BxSxS2_if1, L1_xattn_norm1_w, L1_xattn_norm2_w, L1_xattn_norm3_w, L1_xattn_sa_wq, L1_xattn_sa_wk, L1_xattn_sa_wv, L1_xattn_sa_wo, L1_xattn_ca_wq, L1_xattn_ca_wk, L1_xattn_ca_wv, L1_xattn_ca_wo, L1_xattn_gate_w, L1_xattn_exp_w1, L1_xattn_exp_w2, L1_xattn_sh_w1, L1_xattn_sh_w2)
    return x

_drawn_inputs = setup_inputs


def setup_inputs(seed=0):
    import zlib

    import numpy as np

    out = dict(_drawn_inputs(seed))
    spreads = {'L0_xattn_sa_bq': (0.0, 0.8),
     'L0_xattn_sa_bk': (0.0, 0.8),
     'L0_xattn_sa_bv': (0.0, 0.1),
     'L0_xattn_sa_bo': (0.0, 0.1),
     'L0_xattn_ca_bq': (0.0, 0.8),
     'L0_xattn_ca_bk': (0.0, 0.8),
     'L0_xattn_ca_bv': (0.0, 0.1),
     'L0_xattn_ca_bo': (0.0, 0.1),
     'L0_xattn_ln1_g': (1.0, 0.2),
     'L0_xattn_ln1_b': (0.0, 0.1),
     'L0_xattn_ln2_g': (1.0, 0.2),
     'L0_xattn_ln2_b': (0.0, 0.1),
     'L0_xattn_ln3_g': (1.0, 0.2),
     'L0_xattn_ln3_b': (0.0, 0.1),
     'L0_xattn_router_b': (0.0, 0.1),
     'L0_xattn_e_b1': (0.0, 0.1),
     'L0_xattn_e_b2': (0.0, 0.1),
     'L1_xattn_norm1_w': (1.0, 0.2),
     'L1_xattn_norm2_w': (1.0, 0.2),
     'L1_xattn_norm3_w': (1.0, 0.2)}
    factors = {'L0_xattn_sa_wq': 7.472,
     'L0_xattn_sa_wk': 7.579,
     'L0_xattn_ca_wq': 8.0,
     'L0_xattn_ca_wk': 8.0}
    for name, (base, spread) in spreads.items():
        noise = np.random.default_rng([zlib.crc32(name.encode()), seed]).standard_normal(out[name].shape)
        drawn = base * np.exp(spread * noise) if base else spread * noise
        out[name] = jnp.asarray(drawn.astype(out[name].dtype))
    for name, factor in factors.items():
        out[name] = (out[name] * factor).astype(out[name].dtype)
    return out
```

```python
from contextlib import ExitStack

import numpy as np

import concourse.bass as bass
from concourse import mybir

F32 = mybir.dt.float32
F32R = mybir.dt.float32r
BF16 = mybir.dt.bfloat16
I32 = mybir.dt.int32
U32 = mybir.dt.uint32
ALU = mybir.AluOpType
ACT = mybir.ActivationFunctionType
AX = mybir.AxisListType.X

B, S, D, SK = 16, 256, 128, 1601
H, HD = 16, 8
P = 128
QT = S // P
HG = 4
NG = H // HG
GR = HG * HD
QROWS = 3 * GR
MROW = QROWS
KROWS = QROWS + 1
VW = HD + 1
VCOLS = H * VW
VPAD = 32 - VW
CHUNK = 402
E0, E1, FF, TOPK = 8, 8, 512, 2
NF = FF // P
EPS = 1e-5
BIG = 2.0 ** 100
SCALE = float(1.0 / np.sqrt(np.float32(HD)))
LOOPS = B // 2


def spans(n, step):
    return [(a, min(step, n - a)) for a in range(0, n, step)]


class Counter:

    def __init__(self, ctx, nc, name, step=1):
        self.sem, self.step, self.value = ctx.enter_context(nc.semaphore(name)), step, 0

    def after(self, instruction):
        instruction.then_inc(self.sem, self.step)
        self.value += self.step
        return (self, self.value)


class Ring:

    def __init__(self, buffers):
        self.buffers = buffers
        self.restart()

    def restart(self):
        self.free = [(n, None) for n in range(len(self.buffers))]

    def take(self):
        slot, mark = self.free.pop(0)
        return slot, self.buffers[slot], mark

    def release(self, slot, mark):
        self.free.append((slot, mark))


def until_free(ring):
    while not ring.free:
        yield 0.4


def alternate(*streams):
    now = [0.0] * len(streams)
    live = list(range(len(streams)))
    while live:
        k = min(live, key=lambda n: now[n])
        try:
            now[k] += next(streams[k])
        except StopIteration:
            live.remove(k)
            continue
        yield now[k]


def build(nc, t, out):
    with ExitStack() as ctx:
        program(ctx, nc, t, out)


def program(ctx, nc, t, out):
    pe, dve, act, pool, sp = nc.tensor, nc.vector, nc.scalar, nc.gpsimd, nc.sync

    def sb(name, shape, dtype=F32):
        return ctx.enter_context(nc.sbuf_tensor(name, shape, dtype))

    ident = sb("ident", [P, P])
    ident_b = sb("ident_b", [P, P], BF16)
    head_sel = sb("head_sel", [QROWS, HG])
    iota = sb("iota", [P, E0])
    causal_q = sb("causal_q", [P, QT, S], BF16)
    causal_k = sb("causal_k", [P, QT, S], BF16)
    w_split = sb("w_split", [P, 2, 3, NG, QROWS])
    w_key = sb("w_key", [P, 2, D])
    w_val = sb("w_val", [P, 2, 2, VCOLS])
    w_out = sb("w_out", [P, 2, 2, D])
    b_q = sb("b_q", [QROWS, 2, 3, NG])
    b_k = sb("b_k", [P, 2])
    b_val = sb("b_val", [P, 2, 2, VCOLS])
    rows = sb("rows", [P, 13, D])
    router = sb("router", [P, 2, E0])
    router_b = sb("router_b", [P, E0])
    b_hid = sb("b_hid", [P, E0, NF])
    b_eo = sb("b_eo", [E0, D])
    halves = sb("halves", [P, 2])

    ctxT = sb("ctxT", [P, SK])
    k_hi = sb("k_hi", [P, SK], F32R)
    k_lo = sb("k_lo", [P, SK], F32R)
    mask_int = sb("mask_int", [P, 7 * S], I32)
    probs = Ring([sb(f"probs{n}", [P, HG, S]) for n in range(2)])
    hidden = Ring([sb(f"hidden{n}", [P, NF, S]) for n in range(1)])
    q_diag = Ring([sb(f"q_diag{n}", [KROWS, HG, S], F32R) for n in range(3)])
    experts = Ring([sb(f"expert{n}", [P, 2, FF]) for n in range(2)])
    neg_max_row = Ring([sb(f"neg_max_row{n}", [HG, S], F32R) for n in range(3)])
    junk = sb("junk", [P, 512], BF16)
    cross_bias = Ring([(sb("mask_bias_q", [P, QT, SK], BF16), sb("mask_bias_k", [P, 13, S], BF16))])

    scores = Ring([ctx.enter_context(nc.psum_tensor(f"scores{n}", [P, HG, S], F32)) for n in range(2)])
    small = Ring([ctx.enter_context(nc.psum_tensor(f"small{n}", [P, 512], F32)) for n in range(3)])
    sums = Ring([ctx.enter_context(nc.psum_tensor(f"sums{n}", [P, 512], F32)) for n in range(1)])

    c_pe, c_dve, c_act, c_pool = (Counter(ctx, nc, n) for n in ("c_pe", "c_dve", "c_act", "c_pool"))
    counters = [c_pe, c_dve, c_act, c_pool]

    def dma_counter(name):
        c = Counter(ctx, nc, name, 16)
        counters.append(c)
        return c

    c_ctx, c_kdup, c_mask, c_setup = map(dma_counter, ("c_ctx", "c_kdup", "c_mask", "c_setup"))
    c_expert = [dma_counter(f"c_expert{n}") for n in range(len(experts.buffers))]
    c_maxrow = [dma_counter(f"c_maxrow{n}") for n in range(len(q_diag.buffers))]
    reached = {}

    def wait(engine, *marks):
        for mark in marks:
            if mark is None:
                continue
            counter, value = mark
            key = (id(engine), id(counter))
            if reached.get(key, 0) < value:
                engine.wait_ge(counter.sem, value)
                reached[key] = value

    w_loads = [(ident, "ident"), (head_sel, "head_sel"), (iota, "iota"), (w_split, "w_split"), (w_key, "w_key"), (w_val, "w_val"),
               (w_out, "w_out"), (b_q, "b_q"), (b_k, "b_k"), (b_val, "b_val"), (rows, "rows"),
               (router, "router"), (router_b, "router_b"), (b_hid, "b_hid"), (b_eo, "b_eo"), (halves, "halves")]
    for tile, name in w_loads:
        loaded = c_setup.after(sp.dma_start(tile[:], t[name]))
    for n, name in enumerate(("causal_q", "causal_k")):
        loaded = c_setup.after(sp.dma_start(probs.buffers[n][:, 0:QT, :], t[name]))
    wait(dve, loaded)
    c_dve.after(dve.tensor_copy(causal_q[:], probs.buffers[0][:, 0:QT, :]))
    c_dve.after(dve.tensor_copy(causal_k[:], probs.buffers[1][:, 0:QT, :]))
    c_dve.after(dve.tensor_copy(ident_b[:], ident[:]))

    class Stream:

        def __init__(self, n):
            self.n = n
            self.x = sb(f"x{n}", [P, QT, D])
            self.xT = sb(f"xT{n}", [P, S])
            self.q = sb(f"q{n}", [QROWS, NG, S], F32R)
            self.ks = sb(f"ks{n}", [KROWS, NG, S], F32R)
            self.vs = sb(f"vs{n}", [P, QT * VCOLS + VPAD])
            self.kc = sb(f"kc{n}", [KROWS, NG, SK], F32R)
            self.vc = sb(f"vc{n}", [P, 13 * VCOLS + VPAD])
            self.o = sb(f"o{n}", [P, NG, S])
            self.tmp = sb(f"tmp{n}", [P, QT, D])
            self.tmpT = sb(f"tmpT{n}", [P, S])
            self.chunk_max = sb(f"chunk_max{n}", [P, QT * HG, 4])
            self.neg_max = sb(f"neg_max{n}", [P, QT * HG])
            self.stats = sb(f"stats{n}", [P, QT, 6])
            self.mean_var = sb(f"mean_var{n}", [P, QT, 2])
            self.rstd = sb(f"rstd{n}", [P, QT])
            self.rden = sb(f"rden{n}", [P, QT, H])
            self.lg = sb(f"lg{n}", [P, QT, E0])
            self.top = sb(f"top{n}", [P, QT, 8])
            self.idx = sb(f"idx{n}", [P, QT, 8], U32)
            self.idxf = sb(f"idxf{n}", [P, QT, 8])
            self.gate = sb(f"gate{n}", [P, QT, 4])
            self.pick = sb(f"pick{n}", [P, QT, E0])
            self.comb = sb(f"comb{n}", [P, QT, E0 + 1])
            self.mself_q = sb(f"mself_q{n}", [P, QT, S], BF16)
            self.mself_k = sb(f"mself_k{n}", [P, QT, S], BF16)
            self.c_x = dma_counter(f"c_x{n}")
            self.c_kc = dma_counter(f"c_kc{n}")
            self.c_out = dma_counter(f"c_out{n}")

        def restart(self):
            self.xT_read = self.ks_read = self.vs_read = self.kc_read = self.vc_read = self.q_read = None
            self.neg_max_read = self.o_read = self.tmp_read = self.tmpT_read = self.comb_read = None
            self.group = {}

    streams = [Stream(0), Stream(1)]
    for st in streams:
        c_dve.after(dve.memset(st.ks[MROW:KROWS].bitcast(F32), 1.0))
        c_dve.after(dve.memset(st.kc[MROW:KROWS].bitcast(F32), 1.0))
        c_dve.after(dve.memset(st.vs[:], 0.0))
        c_dve.after(dve.memset(st.vc[:], 0.0))

    nc.all_engine_barrier()
    for c in counters:
        sp.sem_clear(c.sem)
        c.value = 0
    nc.all_engine_barrier()
    reached.clear()
    for ring in (probs, hidden, q_diag, experts, neg_max_row, scores, small, sums, cross_bias):
        ring.restart()

    def transpose_state(st, source, ready):
        slot, ps, free = small.take()
        wait(pe, ready, free)
        for qt in range(QT):
            last = pe.transpose(ps[:, qt * P:(qt + 1) * P], source[:, qt, :], ident[:])
        st.tmp_read = turned = c_pe.after(last)
        wait(act, turned, st.xT_read)
        st.xT_ready = c_act.after(act.activation(st.xT[:], ps[:, 0:S], ACT.Copy))
        small.release(slot, st.xT_ready)

    def inverse_root(st, ready):
        wait(pool, ready)
        return c_pool.after(pool.tensor_tensor(st.rstd[:], st.mean_var[:, :, 1], halves[:], ALU.pow))

    def layer_norm(st, ready, gain, bias):
        wait(dve, ready)
        for qt in range(QT):
            done = c_dve.after(dve.bn_stats(st.stats[:, qt, :], st.x[:, qt, :]))
        wait(dve, done)
        for qt in range(QT):
            done = c_dve.after(dve.bn_aggr(st.mean_var[:, qt, :], st.stats[:, qt, :]))
        wait(dve, done)
        done = c_dve.after(dve.tensor_scalar(st.mean_var[:, :, 1], st.mean_var[:, :, 1], EPS, None, ALU.add))
        rooted = inverse_root(st, done)
        wait(dve, rooted)
        for qt in range(QT):
            done = c_dve.after(dve.tensor_scalar(st.x[:, qt, :], st.x[:, qt, :], st.mean_var[:, qt, 0:1],
                                                 st.rstd[:, qt:qt + 1], ALU.subtract, ALU.mult))
        wait(dve, done)
        done = c_dve.after(dve.tensor_tensor(st.x[:], st.x[:], wide(rows[:, gain, :], QT), ALU.mult))
        wait(dve, done)
        return c_dve.after(dve.tensor_tensor(st.x[:], st.x[:], wide(rows[:, bias, :], QT), ALU.add))

    def wide(ap, n):
        return ap.unsqueeze(1).to_broadcast([ap.shape[0], n, ap.shape[1]])

    def rms_norm(st, ready, gain):
        wait(dve, ready, st.tmp_read)
        for qt in range(QT):
            done = c_dve.after(dve.tensor_tensor_reduce(st.tmp[:, qt, :], st.x[:, qt, :], st.x[:, qt, :], 1.0 / D,
                                                        EPS, ALU.mult, ALU.add, st.mean_var[:, qt, 1:2]))
        rooted = inverse_root(st, done)
        wait(dve, rooted)
        for qt in range(QT):
            done = c_dve.after(dve.scalar_tensor_tensor(
                out=st.tmp[:, qt, :], in0=st.x[:, qt, :], scalar=st.rstd[:, qt:qt + 1], in1=rows[:, gain, :],
                op0=ALU.mult, op1=ALU.mult))
        return done

    def project_split(st, weight, bias, dest, lo_rows, dest_free):
        slot, ps, free = scores.take()
        wait(pe, st.xT_ready, free)
        for g in range(NG):
            last = pe.matmul(ps[0:QROWS, g, :], weight[:, g, :], st.xT[:], start=True, stop=True)
        st.xT_read = projected = c_pe.after(last)
        wait(dve, projected, *dest_free)
        for g in range(NG):
            high = c_dve.after(dve.tensor_scalar(dest[0:QROWS, g, :], ps[0:QROWS, g, :], bias[:, g:g + 1], None,
                                                 ALU.add))
        a, b = lo_rows
        wait(dve, high)
        for g in range(NG):
            done = c_dve.after(dve.scalar_tensor_tensor(
                out=dest[a:b, g, :], in0=ps[a:b, g, :], scalar=bias[a:b, g:g + 1],
                in1=dest[a:b, g, :].bitcast(F32), op0=ALU.add, op1=ALU.subtract))
        scores.release(slot, done)
        return done

    def self_values(st, layer):
        slot, ps, free = small.take()
        wait(pe, st.xT_ready, free)
        for kt in range(QT):
            last = pe.matmul(ps[:, kt * VCOLS:(kt + 1) * VCOLS], st.xT[:, kt * P:(kt + 1) * P],
                             w_val[:, layer, 0, :], start=True, stop=True)
        st.xT_read = made = c_pe.after(last)
        wait(dve, made, st.vs_read)
        n = QT * VCOLS
        done = c_dve.after(dve.tensor_tensor(st.vs[:, 0:n].rearrange("p (k v) -> p k v", k=QT),
                                             ps[:, 0:n].rearrange("p (k v) -> p k v", k=QT),
                                             wide(b_val[:, layer, 0, :], QT), ALU.add))
        small.release(slot, done)
        return done

    def maxima(st, g, keys, keys_ready, n_keys, mask, mask_ready):
        yield from until_free(q_diag)
        slot, qd, free = q_diag.take()
        wait(pool, st.q_ready, free)
        for j in range(HG):
            built = c_pool.after(pool.tensor_scalar(qd[0:QROWS, j, :], st.q[:, g, :].bitcast(F32),
                                                    head_sel[:, j:j + 1], 1.0, ALU.mult, ALU.mult))
        if g == NG - 1:
            st.q_read = built
        wait(pe, built, keys_ready)
        wait(dve, mask_ready, st.neg_max_read)
        parts = [(min(k0, max(n_keys - CHUNK, 0)), min(CHUNK, n_keys)) for k0, _ in spans(n_keys, CHUNK)]
        yield 1.0
        for qt in range(QT):
            for j in range(HG):
                for c, (k0, kn) in enumerate(parts):
                    pslot, ps, pfree = small.take()
                    wait(pe, pfree)
                    made = c_pe.after(pe.matmul(ps[:, 0:kn], qd[0:QROWS, j, qt * P:(qt + 1) * P],
                                                keys[0:QROWS, g, k0:k0 + kn], start=True, stop=True))
                    wait(dve, made)
                    result = st.chunk_max[:, qt * HG + j, c:c + 1]
                    if mask is None:
                        done = dve.tensor_reduce(result, ps[:, 0:kn], AX, ALU.max)
                    else:
                        done = dve.tensor_tensor_reduce(ps[:, 0:kn], ps[:, 0:kn], mask[:, qt, k0:k0 + kn], 1.0,
                                                        -3e38, ALU.add, ALU.max, result)
                    done = c_dve.after(done)
                    small.release(pslot, done)
                    yield 0.45 * kn / CHUNK
        wait(dve, done)
        negated = c_dve.after(dve.tensor_reduce(st.neg_max[:], st.chunk_max[:, :, 0:len(parts)], AX, ALU.max,
                                                negate=True))
        yield 0.5
        pslot, ps, pfree = small.take()
        wait(pe, negated, pfree)
        for qt in range(QT):
            last = pe.transpose(ps[0:HG, qt * P:(qt + 1) * P], st.neg_max[:, qt * HG:(qt + 1) * HG], ident[:])
        st.neg_max_read = turned = c_pe.after(last)
        rslot, row, rfree = neg_max_row.take()
        wait(act, turned, rfree)
        copied = c_act.after(act.activation(row[:], ps[0:HG, 0:S], ACT.Copy))
        small.release(pslot, copied)
        wait(act, copied)
        placed = c_maxrow[slot].after(act.dma_start(qd[MROW:KROWS, :, :].bitcast(F32), row[:].bitcast(F32)))
        neg_max_row.release(rslot, placed)
        st.group[g] = (slot, qd, placed)
        yield 2.0

    def exponentials(st, g, keys, n_keys, values, values_ready, mask):
        slot, qd, placed = st.group[g]
        yield from until_free(sums)
        oslot, acc, ofree = sums.take()
        parts = spans(n_keys, P)
        waiting = []

        def weigh():
            kt, kn, pslot, pr, expd = waiting.pop(0)
            wait(pe, expd)
            if kt == 0:
                wait(pe, ofree, values_ready)
            for j in range(HG):
                v0 = kt * VCOLS + (g * HG + j) * VW
                last = pe.matmul(acc[32 * j:32 * j + 32, 0:S], values[0:kn, v0:v0 + 32], pr[0:kn, j, :],
                                 start=kt == 0, stop=kt == len(parts) - 1)
            st.summed = c_pe.after(last)
            probs.release(pslot, st.summed)

        for kt, (k0, kn) in enumerate(parts):
            sslot, ps, sfree = scores.take()
            wait(pe, placed, sfree)
            for half in range(2):
                pair = slice(2 * half, 2 * half + 2)
                last = pe.matmul(ps[0:kn, pair, :], keys[:, g, k0:k0 + kn], qd[:, pair, :], start=True,
                                 stop=mask is None)
                if mask is not None:
                    last = pe.matmul(ps[0:kn, pair, :], ident_b[0:kn, 0:kn], wide(mask[0:kn, kt, :], 2),
                                     start=False, stop=True)
            st.keys_read = made = c_pe.after(last)
            pslot, pr, pfree = probs.take()
            wait(act, made, pfree)
            expd = c_act.after(act.activation(pr[0:kn], ps[0:kn], ACT.Exp, scale=SCALE))
            scores.release(sslot, expd)
            waiting.append((kt, kn, pslot, pr, expd))
            if len(waiting) > 1:
                weigh()
            yield 1.0
        q_diag.release(slot, st.keys_read)
        weigh()
        wait(act, st.summed, st.o_read)
        st.o_ready = c_act.after(act.activation(st.o[:, g, :], acc[:, 0:S], ACT.Copy))
        sums.release(oslot, st.o_ready)
        yield 0.5

    def attention(st, layer, cross, keys, keys_ready, n_keys, values, values_ready, mask_q, mask_k, mask_ready,
                  bias_row, residual_ready):
        wait(pool, residual_ready)
        st.x_ready = c_pool.after(pool.tensor_tensor(st.x[:], st.x[:], wide(rows[:, bias_row, :], QT), ALU.add))
        yield from maxima(st, 0, keys, keys_ready, n_keys, mask_q, mask_ready)
        wait(pe, mask_ready)
        for g in range(NG):
            steps = [exponentials(st, g, keys, n_keys, values, values_ready, mask_k)]
            if g + 1 < NG:
                steps.append(maxima(st, g + 1, keys, keys_ready, n_keys, mask_q, mask_ready))
            before = 0.0
            for now in alternate(*steps):
                yield max(now - before, 0.0)
                before = max(now, before)
        st.values_read = st.summed
        for qt in range(QT):
            slot, ps, free = small.take()
            wait(pe, st.o_ready, free)
            for g in range(NG):
                last = pe.transpose(ps[:, g * P:(g + 1) * P], st.o[:, g, qt * P:(qt + 1) * P], ident[:])
            st.o_read = turned = c_pe.after(last)
            by_head = ps[:].rearrange("p (h c) -> p h c", h=H)
            wait(dve, turned, st.tmp_read)
            inverted = c_dve.after(dve.reciprocal(st.rden[:, qt, :], by_head[:, :, HD]))
            wait(dve, inverted)
            done = c_dve.after(dve.tensor_tensor(
                st.tmp[:, qt, :].rearrange("p (h c) -> p h c", h=H), by_head[:, :, 0:HD],
                st.rden[:, qt, :].unsqueeze(2).to_broadcast([P, H, HD]), ALU.mult))
            small.release(slot, done)
        yield 2.0
        slot, ps, free = small.take()
        wait(pe, done, free)
        for qt in range(QT):
            last = pe.transpose(ps[:, qt * P:(qt + 1) * P], st.tmp[:, qt, :], ident[:])
        st.tmp_read = turned = c_pe.after(last)
        wait(act, turned, st.tmpT_read)
        copied = c_act.after(act.activation(st.tmpT[:], ps[:, 0:S], ACT.Copy))
        small.release(slot, copied)
        yield 1.5
        slot, ps, free = small.take()
        wait(pe, copied, free)
        for qt in range(QT):
            last = pe.matmul(ps[:, qt * D:(qt + 1) * D], st.tmpT[:, qt * P:(qt + 1) * P],
                             w_out[:, layer, int(cross), :], start=True, stop=True)
        st.tmpT_read = made = c_pe.after(last)
        wait(dve, made, st.x_ready)
        st.x_ready = c_dve.after(dve.tensor_tensor(st.x[:].rearrange("p a d -> p (a d)"), ps[:, 0:QT * D],
                                                   st.x[:].rearrange("p a d -> p (a d)"), ALU.add))
        small.release(slot, st.x_ready)
        yield 1.5

    def self_attention(st, layer, mask_q, mask_k, mask_ready, bias_row, residual_ready):
        k_done = project_split(st, w_split[:, layer, 1], b_q[:, layer, 1, :], st.ks, (GR, 2 * GR), [st.ks_read])
        yield 2.0
        st.q_ready = project_split(st, w_split[:, layer, 0], b_q[:, layer, 0, :], st.q, (2 * GR, 3 * GR),
                                   [st.q_read])
        v_done = self_values(st, layer)
        yield 2.5
        yield from attention(st, layer, False, st.ks, k_done, S, st.vs, v_done, mask_q, mask_k, mask_ready,
                             bias_row, residual_ready)
        st.ks_read = st.keys_read
        st.vs_read = st.values_read

    def cross_attention(st, layer, mask_q, mask_k, mask_ready, bias_row, residual_ready):
        st.q_ready = project_split(st, w_split[:, layer, 2], b_q[:, layer, 2, :], st.q, (2 * GR, 3 * GR),
                                   [st.q_read])
        yield 2.5
        yield from attention(st, layer, True, st.kc, st.kc_ready, SK, st.vc, st.vc_ready, mask_q, mask_k,
                             mask_ready, bias_row, residual_ready)
        st.kc_read = st.keys_read
        st.vc_read = st.values_read

    def context(st, layer, batch):
        wait(sp, shared["ctx_read"])
        loaded = c_ctx.after(sp.dma_start(ctxT[:], t["ctxT"][bass.ds(batch, 1)].rearrange("a p n -> (a p) n")))
        yield 4.0
        for k0, kn in spans(SK, CHUNK):
            slot, ps, free = small.take()
            wait(pe, loaded, free)
            made = c_pe.after(pe.matmul(ps[:, 0:kn], w_key[:, layer, :], ctxT[:, k0:k0 + kn], start=True,
                                        stop=True))
            wait(dve, made, shared["staged_read"])
            high = c_dve.after(dve.tensor_scalar(k_hi[:, k0:k0 + kn], ps[:, 0:kn], b_k[:, layer:layer + 1], None,
                                                 ALU.add))
            wait(dve, high)
            low = c_dve.after(dve.scalar_tensor_tensor(
                out=k_lo[:, k0:k0 + kn], in0=ps[:, 0:kn], scalar=b_k[:, layer:layer + 1],
                in1=k_hi[:, k0:k0 + kn].bitcast(F32), op0=ALU.add, op1=ALU.subtract))
            small.release(slot, low)
            yield 1.2
        wait(sp, low, st.kc_read)
        for g in range(NG):
            for part, source in enumerate((k_hi, k_lo, k_hi)):
                st.kc_ready = st.c_kc.after(sp.dma_start(st.kc[part * GR:(part + 1) * GR, g, :].bitcast(F32),
                                                         source[g * GR:(g + 1) * GR, :].bitcast(F32)))
        shared["staged_read"] = st.kc_ready
        tiles = spans(SK, P)
        for first in range(0, len(tiles), 3):
            some = tiles[first:first + 3]
            kn = some[0][1]
            slot, ps, free = small.take()
            wait(pe, loaded, free)
            for n, (k0, _) in enumerate(some):
                last = pe.matmul(ps[0:kn, n * VCOLS:(n + 1) * VCOLS], ctxT[:, k0:k0 + kn], w_val[:, layer, 1, :],
                                 start=True, stop=True)
            shared["ctx_read"] = made = c_pe.after(last)
            wait(dve, made, st.vc_read)
            w = len(some)
            st.vc_ready = c_dve.after(dve.tensor_tensor(
                st.vc[0:kn, first * VCOLS:(first + w) * VCOLS].rearrange("p (k v) -> p k v", k=w),
                ps[0:kn, 0:w * VCOLS].rearrange("p (k v) -> p k v", k=w),
                wide(b_val[0:kn, layer, 1, :], w), ALU.add))
            small.release(slot, st.vc_ready)
            yield 0.7

    def mask_bias(st, source, dest, dest_free):
        k, n = dest.shape[0], dest.shape[1] * dest.shape[2]
        view = mask_int[0:k, 0:n].rearrange("p (a b) -> p a b", a=dest.shape[1])
        wait(sp, shared["mask_read"])
        loaded = c_mask.after(sp.dma_start(view, source))
        wait(pool, loaded, dest_free)
        shared["mask_read"] = done = c_pool.after(pool.tensor_scalar(dest, view, 0, -BIG, ALU.is_equal, ALU.mult))
        return done

    def self_masks(st, batch):
        b = bass.ds(batch, 1)
        mask_bias(st, t["mself"][b].rearrange("a (q p) k -> (a p) q k", p=P), st.mself_q[:], None)
        yield 3.0
        st.mself_ready = mask_bias(st, t["mselfT"][b].rearrange("a (q p) k -> (a p) q k", p=P), st.mself_k[:],
                                   None)
        yield 3.0

    def cross_masks(st, batch):
        b = bass.ds(batch, 1)
        yield from until_free(cross_bias)
        _, (mask_bias_q, mask_bias_k), masks_read = cross_bias.take()
        st.cross_bias = mask_bias_q, mask_bias_k
        for qt in range(QT):
            mask_bias(st, t["mcross"][b, qt * P:(qt + 1) * P, :].rearrange("a p k -> p a k"),
                      mask_bias_q[:, qt:qt + 1, :], masks_read)
            yield 8.0
        full = SK // P
        for k0, kn in ((0, 6), (6, full - 6)):
            mask_bias(st, t["mcrossT"][b, k0 * P:(k0 + kn) * P, :].rearrange("a (q p) k -> (a p) q k", p=P),
                      mask_bias_k[:, k0:k0 + kn, :], None)
            yield 8.0
        st.mcross_ready = mask_bias(st, t["mcrossT"][b, full * P:SK, :].rearrange("a p k -> p a k"),
                                    mask_bias_k[0:SK - full * P, full:full + 1, :], None)
        yield 3.0

    def route(st, layer, ready):
        slot, ps, free = small.take()
        wait(pe, st.xT_ready, free)
        for qt in range(QT):
            last = pe.matmul(ps[:, qt * E0:(qt + 1) * E0], st.xT[:, qt * P:(qt + 1) * P], router[:, layer, :],
                             start=True, stop=True)
        made = c_pe.after(last)
        wait(dve, made)
        logits = ps[:, 0:QT * E0].rearrange("p (q e) -> p q e", q=QT)
        if layer == 0:
            done = c_dve.after(dve.tensor_tensor(st.lg[:], logits, wide(router_b[:], QT), ALU.add))
        else:
            done = c_dve.after(dve.tensor_copy(st.lg[:], logits))
        small.release(slot, done)
        if layer == 0:
            wait(dve, done)
            done = c_dve.after(dve.tensor_reduce(st.gate[:, :, 0], st.lg[:], AX, ALU.max))
            wait(dve, done)
            done = c_dve.after(dve.tensor_tensor(st.lg[:], st.lg[:],
                                                 st.gate[:, :, 0:1].to_broadcast([P, QT, E0]), ALU.subtract))
            wait(act, done)
            done = c_act.after(act.activation(st.lg[:], st.lg[:], ACT.Exp))
            wait(dve, done)
            done = c_dve.after(dve.tensor_reduce(st.gate[:, :, 0], st.lg[:], AX, ALU.add))
            wait(dve, done)
            done = c_dve.after(dve.reciprocal(st.gate[:, :, 1], st.gate[:, :, 0]))
            wait(dve, done)
            done = c_dve.after(dve.tensor_tensor(st.lg[:], st.lg[:],
                                                 st.gate[:, :, 1:2].to_broadcast([P, QT, E0]), ALU.mult))
        yield 3.0
        wait(dve, done)
        for qt in range(QT):
            done = c_dve.after(dve.max(st.top[:, qt, :], st.lg[:, qt, :]))
        wait(dve, done)
        for qt in range(QT):
            done = c_dve.after(dve.max_index(st.idx[:, qt, :], st.top[:, qt, :], st.lg[:, qt, :]))
        found = done
        done = c_dve.after(dve.tensor_tensor(st.gate[:, :, 2], st.top[:, :, 1], st.top[:, :, 0], ALU.subtract))
        wait(act, done)
        done = c_act.after(act.activation(st.gate[:, :, 2], st.gate[:, :, 2], ACT.Exp))
        wait(dve, found)
        turned = c_dve.after(dve.tensor_copy(st.idxf[:], st.idx[:]))
        wait(dve, done)
        done = c_dve.after(dve.tensor_scalar(st.gate[:, :, 3], st.gate[:, :, 2], 1.0, None, ALU.add))
        wait(dve, done)
        done = c_dve.after(dve.reciprocal(st.gate[:, :, 0], st.gate[:, :, 3]))
        wait(dve, done)
        if layer == 1:
            done = c_dve.after(dve.tensor_scalar(st.gate[:, :, 0], st.gate[:, :, 0], 0.5, None, ALU.mult))
            wait(dve, done)
        done = c_dve.after(dve.tensor_tensor(st.gate[:, :, 1], st.gate[:, :, 0], st.gate[:, :, 2], ALU.mult))
        wait(dve, done, turned, st.comb_read)
        for qt in range(QT):
            done = c_dve.after(dve.tensor_scalar(st.pick[:, qt, :], iota[:], st.idxf[:, qt, 0:1],
                                                 st.gate[:, qt, 0:1], ALU.is_equal, ALU.mult))
            done = c_dve.after(dve.tensor_scalar(st.comb[:, qt, 0:E0], iota[:], st.idxf[:, qt, 1:2],
                                                 st.gate[:, qt, 1:2], ALU.is_equal, ALU.mult))
        wait(dve, done)
        st.comb_ready = c_dve.after(dve.tensor_tensor(st.comb[:, :, 0:E0], st.comb[:, :, 0:E0], st.pick[:],
                                                      ALU.add))
        yield 3.0

    def experts_of(st, layer, residual_ready):
        count = E0 if layer == 0 else E1 + 1
        if layer == 0:
            slot, ps, free = small.take()
            wait(pe, st.comb_ready, free)
            for qt in range(QT):
                last = pe.transpose(ps[0:E0, qt * P:(qt + 1) * P], st.comb[:, qt, 0:E0], ident[:])
            st.comb_read = turned = c_pe.after(last)
            wait(act, turned, st.tmpT_read)
            copied = c_act.after(act.activation(st.tmpT[0:E0, :], ps[0:E0, 0:S], ACT.Copy))
            small.release(slot, copied)
            slot, ps, free = small.take()
            wait(pe, copied, free)
            for qt in range(QT):
                last = pe.matmul(ps[:, qt * D:(qt + 1) * D], st.tmpT[0:E0, qt * P:(qt + 1) * P], b_eo[:],
                                 start=True, stop=True)
            st.tmpT_read = made = c_pe.after(last)
            wait(dve, made, residual_ready)
            flat = st.x[:].rearrange("p a d -> p (a d)")
            residual_ready = c_dve.after(dve.tensor_tensor(flat, ps[:, 0:QT * D], flat, ALU.add))
            small.release(slot, residual_ready)
            yield 2.0
        pending = []

        def second(e, eslot, weights, hslot, hid, ready):
            slot, ps, free = small.take()
            wait(pe, ready, free)
            for qt in range(QT):
                for f in range(NF):
                    last = pe.matmul(ps[:, qt * D:(qt + 1) * D], hid[:, f, qt * P:(qt + 1) * P],
                                     weights[:, 1, f * D:(f + 1) * D], start=f == 0, stop=f == NF - 1)
            made = c_pe.after(last)
            hidden.release(hslot, made)
            experts.release(eslot, made)
            wait(dve, made, st.x_ready, residual_ready, st.comb_ready)
            for qt in range(QT):
                st.x_ready = c_dve.after(dve.scalar_tensor_tensor(
                    out=st.x[:, qt, :], in0=ps[:, qt * D:(qt + 1) * D], scalar=st.comb[:, qt, e:e + 1],
                    in1=st.x[:, qt, :], op0=ALU.mult, op1=ALU.add))
            small.release(slot, st.x_ready)

        for e in range(count):
            yield from until_free(experts)
            eslot, weights, wfree = experts.take()
            wait(sp, wfree)
            loaded = c_expert[eslot].after(sp.dma_start(
                weights[:].rearrange("p a n -> p (a n)"), t["experts"][layer * E0 + e]))
            yield from until_free(hidden)
            slot, ps, free = scores.take()
            wait(pe, loaded, st.xT_ready, free)
            for f in range(NF):
                last = pe.matmul(ps[:, f, :], weights[:, 0, f * P:(f + 1) * P], st.xT[:], start=True, stop=True)
            st.xT_read = made = c_pe.after(last)
            hslot, hid, hfree = hidden.take()
            wait(act, made, hfree)
            if layer == 0:
                for f in range(NF):
                    ready = c_act.after(act.activation(hid[:, f, :], ps[:, f, :], ACT.Gelu,
                                                       bias=b_hid[:, e, f:f + 1]))
            else:
                ready = c_act.after(act.activation(hid[:], ps[:], ACT.Tanh, scale=0.5))
                wait(dve, ready)
                ready = c_dve.after(dve.scalar_tensor_tensor(
                    out=hid[:].rearrange("p a b -> p (a b)"), in0=hid[:].rearrange("p a b -> p (a b)"), scalar=1.0,
                    in1=ps[:].rearrange("p a b -> p (a b)"), op0=ALU.add, op1=ALU.mult))
            scores.release(slot, ready)
            yield 2.0
            second(e, eslot, weights, hslot, hid, ready)
            yield 2.0
        st.comb_read = st.x_ready

    def batch_steps(st, batch):
        st.restart()
        flat = st.x
        loaded = st.c_x.after(sp.dma_start(
            flat[:], t["x"][bass.ds(batch, 1)].rearrange("a (q p) d -> (a p) q d", p=P)))
        prepared = context(st, 0, batch)
        yield next(prepared)
        transpose_state(st, st.x, loaded)
        first = self_attention(st, 0, causal_q, causal_k, None, 0, st.xT_ready)
        yield from blend(first, prepared)
        st.x_ready = layer_norm(st, st.x_ready, 4, 5)
        yield 3.0
        transpose_state(st, st.x, st.x_ready)
        yield from cross_attention(st, 0, None, None, None, 1, st.xT_ready)
        later = [context(st, 1, batch), self_masks(st, batch)]
        if st.n == 0:
            later.append(cross_masks(st, batch))
        st.x_ready = layer_norm(st, st.x_ready, 6, 7)
        yield 3.0
        transpose_state(st, st.x, st.x_ready)
        yield 1.0
        yield from route(st, 0, st.x_ready)
        yield from blend(experts_of(st, 0, st.x_ready), *later[:1])
        st.x_ready = layer_norm(st, st.x_ready, 8, 9)
        yield 3.0
        done = rms_norm(st, st.x_ready, 10)
        yield 2.0
        transpose_state(st, st.tmp, done)
        yield from blend(*later[1:])
        yield from self_attention(st, 1, st.mself_q, st.mself_k, st.mself_ready, 2, done)
        done = rms_norm(st, st.x_ready, 11)
        yield 2.0
        transpose_state(st, st.tmp, done)
        if st.n == 1:
            yield from cross_masks(st, batch)
        yield from cross_attention(st, 1, *st.cross_bias, st.mcross_ready, 3, done)
        cross_bias.release(0, st.keys_read)
        done = rms_norm(st, st.x_ready, 12)
        yield 2.0
        transpose_state(st, st.tmp, done)
        yield 1.0
        yield from route(st, 1, done)
        wait(dve, st.comb_read)
        st.comb_ready = c_dve.after(dve.memset(st.comb[:, :, E1:E1 + 1], 0.5))
        yield from experts_of(st, 1, st.x_ready)
        wait(sp, st.x_ready)
        stored = st.c_out.after(sp.dma_start(
            out[bass.ds(batch, 1)].rearrange("a (q p) d -> (a p) q d", p=P), st.x[:]))
        wait(sp, stored)

    def blend(*steps):
        before = 0.0
        for now in alternate(*steps):
            yield max(now - before, 0.0)
            before = max(now, before)

    with nc.Fori(0, LOOPS) as i:
        shared = {"ctx_read": None, "staged_read": None, "mask_read": None}
        a, b = batch_steps(streams[0], i * 2), batch_steps(streams[1], i * 2 + 1)

        def later(steps, delay):
            yield delay
            yield from steps

        for _ in alternate(a, later(b, OFFSET)):
            pass
        nc.all_engine_barrier()
        for c in counters:
            sp.sem_clear(c.sem)
        nc.all_engine_barrier()


OFFSET = 40.0


def kernel(**inputs):
    import concourse.bacc as bacc
    from concourse.bass_utils import run_bass_kernel_spmd

    a = {k: np.asarray(v) for k, v in inputs.items()}
    f32 = np.float32

    def layer(n):
        return lambda name: a[f"L{n}_xattn_{name}"]

    l0, l1 = layer(0), layer(1)
    zero = np.zeros(D, f32)

    def values(w):
        padded = np.zeros((D, H, VW), f32)
        padded[:, :, :HD] = w.reshape(D, H, HD)
        return padded.reshape(D, VCOLS)

    def value_bias(b):
        padded = np.ones((H, VW), f32)
        padded[:, :HD] = b.reshape(H, HD)
        return np.broadcast_to(padded.reshape(1, VCOLS), (P, VCOLS))

    def thrice(w):
        return np.repeat(w.reshape(D, NG, 1, GR), 3, axis=2).reshape(D, NG, QROWS)

    def row_bias(b):
        return np.tile(b.reshape(NG, GR).T, (3, 1))

    tri = np.tril(np.ones((S, S), bool))
    causal = np.where(tri, f32(0), f32(-BIG)).astype(f32)

    def tiles(m):
        return m.reshape(QT, P, S).transpose(1, 0, 2)

    def expert(w1, w2):
        return np.concatenate([w1, w2.reshape(NF, P, D).transpose(1, 0, 2).reshape(P, NF * D)], axis=1)

    w1s = [l0("e_w1")[e] for e in range(E0)] + [l1("exp_w1")[e].T for e in range(E1)] + [l1("sh_w1").T]
    w2s = [l0("e_w2")[e] for e in range(E0)] + [l1("exp_w2")[e].T for e in range(E1)] + [l1("sh_w2").T]
    arrays = {
        "x": a["x"],
        "ctxT": a["ctx_1024"].transpose(0, 2, 1),
        "mself": a["mask_BxSxS_ik0"],
        "mselfT": a["mask_BxSxS_ik0"].transpose(0, 2, 1),
        "mcross": a["mask_BxSxS2_if1"],
        "mcrossT": a["mask_BxSxS2_if1"].transpose(0, 2, 1),
        "ident": np.eye(P, dtype=f32),
        "head_sel": np.tile(np.kron(np.eye(HG, dtype=f32), np.ones((HD, 1), f32)), (3, 1)),
        "iota": np.broadcast_to(np.arange(E0, dtype=f32), (P, E0)),
        "causal_q": tiles(causal),
        "causal_k": tiles(causal.T),
        "w_split": np.stack([
            np.stack([thrice(l0("sa_wq")), thrice(l0("sa_wk")), thrice(l0("ca_wq"))]),
            np.stack([thrice(l1("sa_wq").T), thrice(l1("sa_wk").T), thrice(l1("ca_wq").T)]),
        ]).transpose(2, 0, 1, 3, 4),
        "w_key": np.stack([l0("ca_wk"), l1("ca_wk").T], axis=1),
        "w_val": np.stack([np.stack([values(l0("sa_wv")), values(l0("ca_wv"))]),
                           np.stack([values(l1("sa_wv").T), values(l1("ca_wv").T)])]).transpose(2, 0, 1, 3),
        "w_out": np.stack([np.stack([l0("sa_wo"), l0("ca_wo")]),
                           np.stack([l1("sa_wo").T, l1("ca_wo").T])]).transpose(2, 0, 1, 3),
        "b_q": np.stack([np.stack([row_bias(l0("sa_bq")), row_bias(l0("sa_bk")), row_bias(l0("ca_bq"))]),
                         np.stack([row_bias(zero)] * 3)]).transpose(2, 0, 1, 3),
        "b_k": np.stack([l0("ca_bk"), zero], axis=1),
        "b_val": np.stack([np.stack([value_bias(l0("sa_bv")), value_bias(l0("ca_bv"))]),
                           np.stack([value_bias(zero)] * 2)]).transpose(2, 0, 1, 3),
        "rows": np.broadcast_to(np.stack([
            l0("sa_bo"), l0("ca_bo"), zero, zero, l0("ln1_g"), l0("ln1_b"), l0("ln2_g"), l0("ln2_b"), l0("ln3_g"),
            l0("ln3_b"), l1("norm1_w"), l1("norm2_w"), l1("norm3_w")]), (P, 13, D)),
        "router": np.stack([l0("router_w"), l1("gate_w").T], axis=1),
        "router_b": np.broadcast_to(l0("router_b"), (P, E0)),
        "b_hid": l0("e_b1").reshape(E0, NF, P).transpose(2, 0, 1),
        "b_eo": l0("e_b2"),
        "halves": np.full((P, 2), -0.5, f32),
        "experts": np.stack([expert(w1, w2) for w1, w2 in zip(w1s, w2s)]),
    }
    arrays = {k: np.ascontiguousarray(v) for k, v in arrays.items()}
    nc = bacc.Bacc("TRN2", target_bir_lowering=False, num_devices=1)
    t = {k: nc.dram_tensor(f"in_{k}", v.shape, mybir.dt.from_np(v.dtype), kind="ExternalInput").ap()
         for k, v in arrays.items()}
    out = nc.dram_tensor("out_x", (B, S, D), F32, kind="ExternalOutput").ap()
    build(nc, t, out)
    r = run_bass_kernel_spmd(nc, [{f"in_{k}": v for k, v in arrays.items()}], core_ids=[0])
    return r.results[0]["out_x"]
```

```python
from contextlib import ExitStack

import numpy as np

import concourse.bass as bass
from concourse import mybir

F32 = mybir.dt.float32
F32R = mybir.dt.float32r
BF16 = mybir.dt.bfloat16
I32 = mybir.dt.int32
U32 = mybir.dt.uint32
ALU = mybir.AluOpType
ACT = mybir.ActivationFunctionType
AX = mybir.AxisListType.X

B, S, D, SK = 16, 256, 128, 1601
H, HD = 16, 8
P = 128
QT = S // P
HG = 4
NG = H // HG
GR = HG * HD
QROWS = 3 * GR
MROW = QROWS
KROWS = QROWS + 1
VW = HD + 1
VCOLS = H * VW
VPAD = 32 - VW
CHUNK = 402
E0, E1, FF, TOPK = 8, 8, 512, 2
NF = FF // P
EPS = 1e-5
BIG = 2.0 ** 100
SCALE = float(1.0 / np.sqrt(np.float32(HD)))
PAIRS = B // 2


def spans(n, step):
    return [(a, min(step, n - a)) for a in range(0, n, step)]


class Counter:

    def __init__(self, ctx, nc, name, clock, engine, step=1, usual=0.2, latency=0.1):
        self.sem, self.step, self.value = ctx.enter_context(nc.semaphore(name)), step, 0
        self.clock, self.engine, self.usual, self.latency = clock, id(engine), usual, latency

    def after(self, instruction, us=None):
        instruction.then_inc(self.sem, self.step)
        self.value += self.step
        self.clock[self.engine] += self.usual if us is None else us
        return (self, self.value, self.clock[self.engine] + self.latency)


class Ring:

    def __init__(self, buffers):
        self.buffers = buffers
        self.restart()

    def restart(self):
        self.free = [(n, None) for n in range(len(self.buffers))]

    def take(self):
        slot, mark = self.free.pop(0)
        return slot, self.buffers[slot], mark

    def release(self, slot, mark):
        self.free.append((slot, mark))

    def next(self):
        return self.free[0][1] if self.free else None


def at(*marks):
    return max((mark[2] for mark in marks if mark is not None), default=0.0)


def alternate(*streams):
    ready = [0.0] * len(streams)
    live = list(range(len(streams)))
    while live:
        k = min(live, key=lambda n: ready[n])
        try:
            ready[k] = next(streams[k])
        except StopIteration:
            live.remove(k)
            continue
        yield min(ready[n] for n in live)


def chain(*steps):
    for one in steps:
        yield from one


def build(nc, t, out):
    with ExitStack() as ctx:
        program(ctx, nc, t, out)


def program(ctx, nc, t, out):
    pe, dve, act, pool, sp = nc.tensor, nc.vector, nc.scalar, nc.gpsimd, nc.sync

    def sb(name, shape, dtype=F32):
        return ctx.enter_context(nc.sbuf_tensor(name, shape, dtype))

    ident = sb("ident", [P, P])
    ident_b = sb("ident_b", [P, P], BF16)
    head_sel = sb("head_sel", [QROWS, HG])
    iota = sb("iota", [P, E0])
    causal_q = sb("causal_q", [P, QT, S], BF16)
    causal_k = sb("causal_k", [P, QT, S], BF16)
    w_split = sb("w_split", [P, 2, 3, NG, QROWS])
    w_key = sb("w_key", [P, 2, D])
    w_val = sb("w_val", [P, 2, 2, VCOLS])
    w_out = sb("w_out", [P, 2, 2, D])
    b_q = sb("b_q", [QROWS, 2, 3, NG])
    b_k = sb("b_k", [P, 2])
    b_val = sb("b_val", [P, 2, 2, VCOLS])
    rows = sb("rows", [P, 13, D])
    router = sb("router", [P, 2, E0])
    router_b = sb("router_b", [P, E0])
    b_hid = sb("b_hid", [P, E0, NF])
    b_eo = sb("b_eo", [E0, D])
    halves = sb("halves", [P, 2])

    context_in = Ring([sb("ctxT", [P, SK])])
    split_keys = Ring([(sb("k_hi", [P, SK], F32R), sb("k_lo", [P, SK], F32R))])
    mask_words = Ring([sb("mask_words", [P, 7 * S], I32)])
    probs = Ring([sb(f"probs{n}", [P, HG, S]) for n in range(3)])
    hidden = Ring([sb(f"hidden{n}", [P, NF, S]) for n in range(2)])
    q_diag = Ring([sb(f"q_diag{n}", [KROWS, HG, S], F32R) for n in range(3)])
    experts = Ring([sb(f"expert{n}", [P, 2, FF]) for n in range(3)])
    neg_max_row = Ring([sb(f"neg_max_row{n}", [HG, S], F32R) for n in range(3)])
    junk = sb("junk", [P, 512], BF16)
    mask_bias_q, mask_bias_k = sb("mask_bias_q", [P, QT, SK], BF16), sb("mask_bias_k", [P, 13, S], BF16)
    cross_bias = Ring([(mask_bias_q, mask_bias_k)])

    scores = Ring([ctx.enter_context(nc.psum_tensor(f"scores{n}", [P, HG, S], F32)) for n in range(2)])
    small = Ring([ctx.enter_context(nc.psum_tensor(f"small{n}", [P, 512], F32)) for n in range(3)])
    sums = Ring([ctx.enter_context(nc.psum_tensor(f"sums{n}", [P, 512], F32)) for n in range(1)])

    clock = {id(engine): 0.0 for engine in (pe, dve, act, pool, sp)}
    c_pe = Counter(ctx, nc, "c_pe", clock, pe, usual=0.3)
    c_dve = Counter(ctx, nc, "c_dve", clock, dve)
    c_act = Counter(ctx, nc, "c_act", clock, act, usual=0.45)
    c_pool = Counter(ctx, nc, "c_pool", clock, pool, usual=0.5)
    counters = [c_pe, c_dve, c_act, c_pool]

    def dma_counter(name, engine=sp, latency=2.5):
        c = Counter(ctx, nc, name, clock, engine, 16, usual=0.05, latency=latency)
        counters.append(c)
        return c

    c_ctx, c_mask, c_setup = dma_counter("c_ctx", latency=7.0), dma_counter("c_mask", latency=7.0), dma_counter("c_setup")
    c_expert = [dma_counter(f"c_expert{n}", latency=5.0) for n in range(len(experts.buffers))]
    c_maxrow = [dma_counter(f"c_maxrow{n}", act) for n in range(len(q_diag.buffers))]
    reached = {}

    def wait(engine, *marks):
        for mark in marks:
            if mark is None:
                continue
            counter, value, time = mark
            key = (id(engine), id(counter))
            if reached.get(key, 0) < value:
                engine.wait_ge(counter.sem, value)
                reached[key] = value
            clock[id(engine)] = max(clock[id(engine)], time)

    w_loads = [(ident, "ident"), (head_sel, "head_sel"), (iota, "iota"), (w_split, "w_split"), (w_key, "w_key"), (w_val, "w_val"),
               (w_out, "w_out"), (b_q, "b_q"), (b_k, "b_k"), (b_val, "b_val"), (rows, "rows"),
               (router, "router"), (router_b, "router_b"), (b_hid, "b_hid"), (b_eo, "b_eo"), (halves, "halves")]
    for tile, name in w_loads:
        loaded = c_setup.after(sp.dma_start(tile[:], t[name]))
    for n, name in enumerate(("causal_q", "causal_k")):
        loaded = c_setup.after(sp.dma_start(probs.buffers[n][:, 0:QT, :], t[name]))
    wait(dve, loaded)
    c_dve.after(dve.tensor_copy(causal_q[:], probs.buffers[0][:, 0:QT, :]))
    c_dve.after(dve.tensor_copy(causal_k[:], probs.buffers[1][:, 0:QT, :]))
    c_dve.after(dve.tensor_copy(ident_b[:], ident[:]))

    class Stream:

        def __init__(self, n):
            self.n = n
            self.x = sb(f"x{n}", [P, QT, D])
            self.xT = sb(f"xT{n}", [P, S])
            self.q = sb(f"q{n}", [QROWS, NG, S], F32R)
            self.ks = sb(f"ks{n}", [KROWS, NG, S], F32R)
            self.vs = sb(f"vs{n}", [P, QT * VCOLS + VPAD])
            self.kc = sb(f"kc{n}", [KROWS, NG, SK], F32R)
            self.vc = sb(f"vc{n}", [P, 13 * VCOLS + VPAD])
            self.o = sb(f"o{n}", [P, NG, S])
            self.tmp = sb(f"tmp{n}", [P, QT, D])
            self.tmpT = sb(f"tmpT{n}", [P, S])
            self.chunk_max = sb(f"chunk_max{n}", [P, QT * HG, 4])
            self.neg_max = sb(f"neg_max{n}", [P, QT * HG])
            self.stats = sb(f"stats{n}", [P, QT, 6])
            self.mean_var = sb(f"mean_var{n}", [P, QT, 2])
            self.rstd = sb(f"rstd{n}", [P, QT])
            self.rden = sb(f"rden{n}", [P, QT, H])
            self.lg = sb(f"lg{n}", [P, QT, E0])
            self.top = sb(f"top{n}", [P, QT, 8])
            self.idx = sb(f"idx{n}", [P, QT, 8], U32)
            self.idxf = sb(f"idxf{n}", [P, QT, 8])
            self.gate = sb(f"gate{n}", [P, QT, 4])
            self.pick = sb(f"pick{n}", [P, QT, E0])
            self.comb = sb(f"comb{n}", [P, QT, E0 + 1])
            self.mself_q = sb(f"mself_q{n}", [P, QT, S], BF16)
            self.mself_k = sb(f"mself_k{n}", [P, QT, S], BF16)
            self.c_x = dma_counter(f"c_x{n}")
            self.c_kc = dma_counter(f"c_kc{n}", latency=8.0)
            self.c_out = dma_counter(f"c_out{n}")

        def restart(self):
            self.xT_read = self.ks_read = self.vs_read = self.kc_read = self.vc_read = self.q_read = None
            self.neg_max_read = self.o_read = self.tmp_read = self.tmpT_read = self.comb_read = None
            self.x_ready = self.xT_ready = self.comb_ready = self.kc_ready = self.vc_ready = None
            self.mself_ready = self.mcross_ready = self.mself_read = None
            self.group = {}

    streams = [Stream(0), Stream(1)]
    for st in streams:
        c_dve.after(dve.memset(st.ks[MROW:KROWS].bitcast(F32), 1.0))
        c_dve.after(dve.memset(st.kc[MROW:KROWS].bitcast(F32), 1.0))
        c_dve.after(dve.memset(st.vs[:], 0.0))
        c_dve.after(dve.memset(st.vc[:], 0.0))

    def restart():
        nc.all_engine_barrier()
        for c in counters:
            sp.sem_clear(c.sem)
            c.value = 0
        nc.all_engine_barrier()
        reached.clear()
        for ring in (probs, hidden, q_diag, experts, neg_max_row, scores, small, sums, context_in, split_keys,
                     mask_words):
            ring.restart()
        for st in streams:
            st.restart()
        for engine in clock:
            clock[engine] = 0.0

    restart()

    def until_free(ring):
        later = 0.0
        while not ring.free:
            later = max(later, clock[id(pe)]) + 0.5
            yield later

    def transpose_state(st, source, ready):
        yield at(ready, small.next())
        slot, ps, free = small.take()
        wait(pe, ready, free)
        for qt in range(QT):
            last = pe.transpose(ps[:, qt * P:(qt + 1) * P], source[:, qt, :], ident[:])
        st.tmp_read = turned = c_pe.after(last, 0.45)
        wait(act, turned, st.xT_read)
        st.xT_ready = c_act.after(act.activation(st.xT[:], ps[:, 0:S], ACT.Copy), 0.36)
        small.release(slot, st.xT_ready)

    def inverse_root(st, ready):
        wait(pool, ready)
        return c_pool.after(pool.tensor_tensor(st.rstd[:], st.mean_var[:, :, 1], halves[:], ALU.pow))

    def layer_norm(st, ready, gain, bias):
        wait(dve, ready)
        for qt in range(QT):
            done = c_dve.after(dve.bn_stats(st.stats[:, qt, :], st.x[:, qt, :]))
        wait(dve, done)
        for qt in range(QT):
            done = c_dve.after(dve.bn_aggr(st.mean_var[:, qt, :], st.stats[:, qt, :]))
        wait(dve, done)
        done = c_dve.after(dve.tensor_scalar(st.mean_var[:, :, 1], st.mean_var[:, :, 1], EPS, None, ALU.add))
        rooted = inverse_root(st, done)
        yield at(rooted)
        wait(dve, rooted)
        for qt in range(QT):
            done = c_dve.after(dve.tensor_scalar(st.x[:, qt, :], st.x[:, qt, :], st.mean_var[:, qt, 0:1],
                                                 st.rstd[:, qt:qt + 1], ALU.subtract, ALU.mult))
        wait(dve, done)
        done = c_dve.after(dve.tensor_tensor(st.x[:], st.x[:], wide(rows[:, gain, :], QT), ALU.mult))
        wait(dve, done)
        st.x_ready = c_dve.after(dve.tensor_tensor(st.x[:], st.x[:], wide(rows[:, bias, :], QT), ALU.add), 0.3)

    def wide(ap, n):
        return ap.unsqueeze(1).to_broadcast([ap.shape[0], n, ap.shape[1]])

    def rms_norm(st, ready, gain):
        wait(dve, ready, st.tmp_read)
        for qt in range(QT):
            done = c_dve.after(dve.tensor_tensor_reduce(st.tmp[:, qt, :], st.x[:, qt, :], st.x[:, qt, :], 1.0 / D,
                                                        EPS, ALU.mult, ALU.add, st.mean_var[:, qt, 1:2]))
        rooted = inverse_root(st, done)
        yield at(rooted)
        wait(dve, rooted)
        for qt in range(QT):
            done = c_dve.after(dve.scalar_tensor_tensor(
                out=st.tmp[:, qt, :], in0=st.x[:, qt, :], scalar=st.rstd[:, qt:qt + 1], in1=rows[:, gain, :],
                op0=ALU.mult, op1=ALU.mult))
        st.normed = done

    def project_split(st, weight, bias, dest, lo_rows, dest_free):
        slot, ps, free = scores.take()
        wait(pe, st.xT_ready, free)
        for g in range(NG):
            last = pe.matmul(ps[0:QROWS, g, :], weight[:, g, :], st.xT[:], start=True, stop=True)
        st.xT_read = projected = c_pe.after(last, 1.8)
        wait(dve, projected, *dest_free)
        for g in range(NG):
            high = c_dve.after(dve.tensor_scalar(dest[0:QROWS, g, :], ps[0:QROWS, g, :], bias[:, g:g + 1], None,
                                                 ALU.add), 0.33)
        a, b = lo_rows
        wait(dve, high)
        for g in range(NG):
            done = c_dve.after(dve.scalar_tensor_tensor(
                out=dest[a:b, g, :], in0=ps[a:b, g, :], scalar=bias[a:b, g:g + 1],
                in1=dest[a:b, g, :].bitcast(F32), op0=ALU.add, op1=ALU.subtract), 0.33)
        scores.release(slot, done)
        return done

    def self_values(st, layer):
        slot, ps, free = small.take()
        wait(pe, st.xT_ready, free)
        for kt in range(QT):
            last = pe.matmul(ps[:, kt * VCOLS:(kt + 1) * VCOLS], st.xT[:, kt * P:(kt + 1) * P],
                             w_val[:, layer, 0, :], start=True, stop=True)
        st.xT_read = made = c_pe.after(last, 0.5)
        wait(dve, made, st.vs_read)
        n = QT * VCOLS
        done = c_dve.after(dve.tensor_tensor(st.vs[:, 0:n].rearrange("p (k v) -> p k v", k=QT),
                                             ps[:, 0:n].rearrange("p (k v) -> p k v", k=QT),
                                             wide(b_val[:, layer, 0, :], QT), ALU.add), 0.4)
        small.release(slot, done)
        return done

    def maxima(st, g, keys, keys_ready, n_keys, mask, mask_ready):
        yield from until_free(q_diag)
        slot, qd, free = q_diag.take()
        yield at(st.q_ready, free)
        wait(pool, st.q_ready, free)
        for j in range(HG):
            built = c_pool.after(pool.tensor_scalar(qd[0:QROWS, j, :], st.q[:, g, :].bitcast(F32),
                                                    head_sel[:, j:j + 1], 1.0, ALU.mult, ALU.mult), 0.46)
        if g == NG - 1:
            st.q_read = built
        parts = [(min(k0, max(n_keys - CHUNK, 0)), min(CHUNK, n_keys)) for k0, _ in spans(n_keys, CHUNK)]
        for qt in range(QT):
            for j in range(HG):
                for c, (k0, kn) in enumerate(parts):
                    yield at(built, keys_ready, small.next())
                    pslot, ps, pfree = small.take()
                    wait(pe, built, keys_ready, pfree)
                    made = c_pe.after(pe.matmul(ps[:, 0:kn], qd[0:QROWS, j, qt * P:(qt + 1) * P],
                                                keys[0:QROWS, g, k0:k0 + kn], start=True, stop=True), 0.5 * kn / 1000)
                    wait(dve, made, mask_ready, st.neg_max_read)
                    result = st.chunk_max[:, qt * HG + j, c:c + 1]
                    if mask is None:
                        done = dve.tensor_reduce(result, ps[:, 0:kn], AX, ALU.max)
                    else:
                        done = dve.tensor_tensor_reduce(ps[:, 0:kn], ps[:, 0:kn], mask[:, qt, k0:k0 + kn], 1.0,
                                                        -3e38, ALU.add, ALU.max, result)
                    done = c_dve.after(done, 0.08 + kn / 960)
                    small.release(pslot, done)
        wait(dve, done)
        negated = c_dve.after(dve.tensor_reduce(st.neg_max[:], st.chunk_max[:, :, 0:len(parts)], AX, ALU.max,
                                                negate=True))
        yield at(negated, small.next())
        pslot, ps, pfree = small.take()
        wait(pe, negated, pfree)
        for qt in range(QT):
            last = pe.transpose(ps[0:HG, qt * P:(qt + 1) * P], st.neg_max[:, qt * HG:(qt + 1) * HG], ident[:])
        st.neg_max_read = turned = c_pe.after(last)
        rslot, row, rfree = neg_max_row.take()
        wait(act, turned, rfree)
        copied = c_act.after(act.activation(row[:], ps[0:HG, 0:S], ACT.Copy))
        small.release(pslot, copied)
        wait(act, copied)
        placed = c_maxrow[slot].after(act.dma_start(qd[MROW:KROWS, :, :].bitcast(F32), row[:].bitcast(F32)))
        neg_max_row.release(rslot, placed)
        st.group[g] = (slot, qd, placed)

    def exponentials(st, g, keys, n_keys, values, values_ready, mask):
        slot, qd, placed = st.group[g]
        yield from until_free(sums)
        oslot, acc, ofree = sums.take()
        parts = spans(n_keys, P)
        waiting = []

        def weigh():
            kt, kn, pslot, pr, expd = waiting.pop(0)
            wait(pe, expd)
            if kt == 0:
                wait(pe, ofree, values_ready)
            for j in range(HG):
                v0 = kt * VCOLS + (g * HG + j) * VW
                last = pe.matmul(acc[32 * j:32 * j + 32, 0:S], values[0:kn, v0:v0 + 32], pr[0:kn, j, :],
                                 start=kt == 0, stop=kt == len(parts) - 1)
            st.summed = c_pe.after(last, 0.52)
            probs.release(pslot, st.summed)

        for kt, (k0, kn) in enumerate(parts):
            yield at(placed, scores.next())
            sslot, ps, sfree = scores.take()
            wait(pe, placed, sfree)
            for half in range(2):
                pair = slice(2 * half, 2 * half + 2)
                last = pe.matmul(ps[0:kn, pair, :], keys[:, g, k0:k0 + kn], qd[:, pair, :], start=True,
                                 stop=mask is None)
                if mask is not None:
                    last = pe.matmul(ps[0:kn, pair, :], ident_b[0:kn, 0:kn], wide(mask[0:kn, kt, :], 2),
                                     start=False, stop=True)
            st.keys_read = made = c_pe.after(last, 0.44 if mask is None else 0.88)
            pslot, pr, pfree = probs.take()
            wait(act, made, pfree)
            expd = c_act.after(act.activation(pr[0:kn], ps[0:kn], ACT.Exp, scale=SCALE), 0.9)
            scores.release(sslot, expd)
            waiting.append((kt, kn, pslot, pr, expd))
            if len(waiting) > 1:
                yield at(waiting[0][4], ofree, values_ready)
                weigh()
        q_diag.release(slot, st.keys_read)
        yield at(expd, ofree, values_ready)
        weigh()
        wait(act, st.summed, st.o_read)
        st.o_ready = c_act.after(act.activation(st.o[:, g, :], acc[:, 0:S], ACT.Copy))
        sums.release(oslot, st.o_ready)

    def attention(st, layer, cross, keys, keys_ready, n_keys, values, values_ready, mask_q, mask_k, mask_ready,
                  bias_row, residual_ready):
        wait(pool, residual_ready)
        st.x_ready = c_pool.after(pool.tensor_tensor(st.x[:], st.x[:], wide(rows[:, bias_row, :], QT), ALU.add))
        yield from maxima(st, 0, keys, keys_ready, n_keys, mask_q, mask_ready)
        wait(pe, mask_ready)
        for g in range(NG):
            steps = [exponentials(st, g, keys, n_keys, values, values_ready, mask_k)]
            if g + 1 < NG:
                steps.append(maxima(st, g + 1, keys, keys_ready, n_keys, mask_q, mask_ready))
            yield from alternate(*steps)
        st.values_read = st.summed
        for qt in range(QT):
            yield at(st.o_ready, small.next())
            slot, ps, free = small.take()
            wait(pe, st.o_ready, free)
            for g in range(NG):
                last = pe.transpose(ps[:, g * P:(g + 1) * P], st.o[:, g, qt * P:(qt + 1) * P], ident[:])
            st.o_read = turned = c_pe.after(last, 0.9)
            by_head = ps[:].rearrange("p (h c) -> p h c", h=H)
            wait(dve, turned, st.tmp_read)
            inverted = c_dve.after(dve.reciprocal(st.rden[:, qt, :], by_head[:, :, HD]))
            wait(dve, inverted)
            done = c_dve.after(dve.tensor_tensor(
                st.tmp[:, qt, :].rearrange("p (h c) -> p h c", h=H), by_head[:, :, 0:HD],
                st.rden[:, qt, :].unsqueeze(2).to_broadcast([P, H, HD]), ALU.mult))
            small.release(slot, done)
        yield at(done, small.next())
        slot, ps, free = small.take()
        wait(pe, done, free)
        for qt in range(QT):
            last = pe.transpose(ps[:, qt * P:(qt + 1) * P], st.tmp[:, qt, :], ident[:])
        st.tmp_read = turned = c_pe.after(last)
        wait(act, turned, st.tmpT_read)
        copied = c_act.after(act.activation(st.tmpT[:], ps[:, 0:S], ACT.Copy))
        small.release(slot, copied)
        yield at(copied, small.next())
        slot, ps, free = small.take()
        wait(pe, copied, free)
        for qt in range(QT):
            last = pe.matmul(ps[:, qt * D:(qt + 1) * D], st.tmpT[:, qt * P:(qt + 1) * P],
                             w_out[:, layer, int(cross), :], start=True, stop=True)
        st.tmpT_read = made = c_pe.after(last)
        wait(dve, made, st.x_ready)
        st.x_ready = c_dve.after(dve.tensor_tensor(st.x[:].rearrange("p a d -> p (a d)"), ps[:, 0:QT * D],
                                                   st.x[:].rearrange("p a d -> p (a d)"), ALU.add))
        small.release(slot, st.x_ready)

    def self_attention(st, layer, mask_q, mask_k, mask_ready, bias_row, residual_ready):
        yield at(st.xT_ready, scores.next())
        k_done = project_split(st, w_split[:, layer, 1], b_q[:, layer, 1, :], st.ks, (GR, 2 * GR), [st.ks_read])
        yield at(scores.next())
        st.q_ready = project_split(st, w_split[:, layer, 0], b_q[:, layer, 0, :], st.q, (2 * GR, 3 * GR),
                                   [st.q_read])
        v_done = self_values(st, layer)
        yield from attention(st, layer, False, st.ks, k_done, S, st.vs, v_done, mask_q, mask_k, mask_ready,
                             bias_row, residual_ready)
        st.ks_read = st.keys_read
        st.vs_read = st.values_read

    def cross_attention(st, layer, mask_q, mask_k, mask_ready, bias_row, residual_ready):
        yield at(st.xT_ready, scores.next())
        st.q_ready = project_split(st, w_split[:, layer, 2], b_q[:, layer, 2, :], st.q, (2 * GR, 3 * GR),
                                   [st.q_read])
        yield from attention(st, layer, True, st.kc, st.kc_ready, SK, st.vc, st.vc_ready, mask_q, mask_k,
                             mask_ready, bias_row, residual_ready)
        st.kc_read = st.keys_read
        st.vc_read = st.values_read

    def context(st, layer, batch):
        yield from until_free(context_in)
        cslot, ctxT, cfree = context_in.take()
        wait(sp, cfree)
        loaded = c_ctx.after(sp.dma_start(ctxT[:], t["ctxT"][bass.ds(batch, 1)].rearrange("a p n -> (a p) n")))
        yield from until_free(split_keys)
        kslot, (k_hi, k_lo), kfree = split_keys.take()
        for k0, kn in spans(SK, CHUNK):
            yield at(loaded, kfree, small.next())
            slot, ps, free = small.take()
            wait(pe, loaded, free)
            made = c_pe.after(pe.matmul(ps[:, 0:kn], w_key[:, layer, :], ctxT[:, k0:k0 + kn], start=True,
                                        stop=True), 0.75)
            wait(dve, made, kfree)
            high = c_dve.after(dve.tensor_scalar(k_hi[:, k0:k0 + kn], ps[:, 0:kn], b_k[:, layer:layer + 1], None,
                                                 ALU.add), 0.5)
            wait(dve, high)
            low = c_dve.after(dve.scalar_tensor_tensor(
                out=k_lo[:, k0:k0 + kn], in0=ps[:, 0:kn], scalar=b_k[:, layer:layer + 1],
                in1=k_hi[:, k0:k0 + kn].bitcast(F32), op0=ALU.add, op1=ALU.subtract), 0.55)
            small.release(slot, low)
        wait(sp, low, st.kc_read)
        for g in range(NG):
            for part, source in enumerate((k_hi, k_lo, k_hi)):
                st.kc_ready = st.c_kc.after(sp.dma_start(st.kc[part * GR:(part + 1) * GR, g, :].bitcast(F32),
                                                         source[g * GR:(g + 1) * GR, :].bitcast(F32)))
        split_keys.release(kslot, st.kc_ready)
        tiles = spans(SK, P)
        for first in range(0, len(tiles), 3):
            some = tiles[first:first + 3]
            kn = some[0][1]
            yield at(loaded, small.next())
            slot, ps, free = small.take()
            wait(pe, loaded, free)
            for n, (k0, _) in enumerate(some):
                last = pe.matmul(ps[0:kn, n * VCOLS:(n + 1) * VCOLS], ctxT[:, k0:k0 + kn], w_val[:, layer, 1, :],
                                 start=True, stop=True)
            made = c_pe.after(last, 0.8)
            wait(dve, made, st.vc_read)
            w = len(some)
            st.vc_ready = c_dve.after(dve.tensor_tensor(
                st.vc[0:kn, first * VCOLS:(first + w) * VCOLS].rearrange("p (k v) -> p k v", k=w),
                ps[0:kn, 0:w * VCOLS].rearrange("p (k v) -> p k v", k=w),
                wide(b_val[0:kn, layer, 1, :], w), ALU.add), 0.55)
            small.release(slot, st.vc_ready)
        context_in.release(cslot, made)

    def mask_bias(st, source, dest, dest_free):
        k, n = dest.shape[0], dest.shape[1] * dest.shape[2]
        yield from until_free(mask_words)
        slot, words, free = mask_words.take()
        view = words[0:k, 0:n].rearrange("p (a b) -> p a b", a=dest.shape[1])
        wait(sp, free)
        loaded = c_mask.after(sp.dma_start(view, source))
        yield at(loaded)
        wait(dve, loaded, dest_free)
        done = c_dve.after(dve.tensor_scalar(dest, view, 0, -BIG, ALU.is_equal, ALU.mult), 1.0)
        mask_words.release(slot, done)
        st.masked = done

    def masks(st, batch):
        b = bass.ds(batch, 1)
        yield from mask_bias(st, t["mself"][b].rearrange("a (q p) k -> (a p) q k", p=P), st.mself_q[:],
                  st.mself_read)
        yield from mask_bias(st, t["mselfT"][b].rearrange("a (q p) k -> (a p) q k", p=P), st.mself_k[:],
                                   None)
        st.mself_ready = st.masked
        yield from until_free(cross_bias)
        _, _, masks_read = cross_bias.take()
        for qt in range(QT):
            yield at(masks_read)
            yield from mask_bias(st, t["mcross"][b, qt * P:(qt + 1) * P, :].rearrange("a p k -> p a k"),
                      mask_bias_q[:, qt:qt + 1, :], masks_read)
        full = SK // P
        for k0, kn in ((0, 6), (6, full - 6)):
            yield from mask_bias(st, t["mcrossT"][b, k0 * P:(k0 + kn) * P, :].rearrange("a (q p) k -> (a p) q k", p=P),
                      mask_bias_k[:, k0:k0 + kn, :], None)
        yield from mask_bias(st, t["mcrossT"][b, full * P:SK, :].rearrange("a p k -> p a k"),
                                    mask_bias_k[0:SK - full * P, full:full + 1, :], None)
        st.mcross_ready = st.masked

    def route(st, layer, ready):
        yield at(st.xT_ready, small.next())
        slot, ps, free = small.take()
        wait(pe, st.xT_ready, free)
        for qt in range(QT):
            last = pe.matmul(ps[:, qt * E0:(qt + 1) * E0], st.xT[:, qt * P:(qt + 1) * P], router[:, layer, :],
                             start=True, stop=True)
        made = c_pe.after(last)
        wait(dve, made)
        logits = ps[:, 0:QT * E0].rearrange("p (q e) -> p q e", q=QT)
        if layer == 0:
            done = c_dve.after(dve.tensor_tensor(st.lg[:], logits, wide(router_b[:], QT), ALU.add))
        else:
            done = c_dve.after(dve.tensor_copy(st.lg[:], logits))
        small.release(slot, done)
        if layer == 0:
            wait(dve, done)
            done = c_dve.after(dve.tensor_reduce(st.gate[:, :, 0], st.lg[:], AX, ALU.max))
            wait(dve, done)
            done = c_dve.after(dve.tensor_tensor(st.lg[:], st.lg[:],
                                                 st.gate[:, :, 0:1].to_broadcast([P, QT, E0]), ALU.subtract))
            wait(act, done)
            done = c_act.after(act.activation(st.lg[:], st.lg[:], ACT.Exp))
            yield at(done)
            wait(dve, done)
            done = c_dve.after(dve.tensor_reduce(st.gate[:, :, 0], st.lg[:], AX, ALU.add))
            wait(dve, done)
            done = c_dve.after(dve.reciprocal(st.gate[:, :, 1], st.gate[:, :, 0]))
            wait(dve, done)
            done = c_dve.after(dve.tensor_tensor(st.lg[:], st.lg[:],
                                                 st.gate[:, :, 1:2].to_broadcast([P, QT, E0]), ALU.mult))
        wait(dve, done)
        for qt in range(QT):
            done = c_dve.after(dve.max(st.top[:, qt, :], st.lg[:, qt, :]))
        wait(dve, done)
        for qt in range(QT):
            done = c_dve.after(dve.max_index(st.idx[:, qt, :], st.top[:, qt, :], st.lg[:, qt, :]))
        found = done
        done = c_dve.after(dve.tensor_tensor(st.gate[:, :, 2], st.top[:, :, 1], st.top[:, :, 0], ALU.subtract))
        wait(act, done)
        done = c_act.after(act.activation(st.gate[:, :, 2], st.gate[:, :, 2], ACT.Exp))
        wait(dve, found)
        turned = c_dve.after(dve.tensor_copy(st.idxf[:], st.idx[:]))
        yield at(done)
        wait(dve, done)
        done = c_dve.after(dve.tensor_scalar(st.gate[:, :, 3], st.gate[:, :, 2], 1.0, None, ALU.add))
        wait(dve, done)
        done = c_dve.after(dve.reciprocal(st.gate[:, :, 0], st.gate[:, :, 3]))
        wait(dve, done)
        if layer == 1:
            done = c_dve.after(dve.tensor_scalar(st.gate[:, :, 0], st.gate[:, :, 0], 0.5, None, ALU.mult))
            wait(dve, done)
        done = c_dve.after(dve.tensor_tensor(st.gate[:, :, 1], st.gate[:, :, 0], st.gate[:, :, 2], ALU.mult))
        wait(dve, done, turned, st.comb_read)
        for qt in range(QT):
            done = c_dve.after(dve.tensor_scalar(st.pick[:, qt, :], iota[:], st.idxf[:, qt, 0:1],
                                                 st.gate[:, qt, 0:1], ALU.is_equal, ALU.mult))
            done = c_dve.after(dve.tensor_scalar(st.comb[:, qt, 0:E0], iota[:], st.idxf[:, qt, 1:2],
                                                 st.gate[:, qt, 1:2], ALU.is_equal, ALU.mult))
        wait(dve, done)
        st.comb_ready = c_dve.after(dve.tensor_tensor(st.comb[:, :, 0:E0], st.comb[:, :, 0:E0], st.pick[:],
                                                      ALU.add))

    def experts_of(st, layer, residual_ready):
        count = E0 if layer == 0 else E1 + 1
        if layer == 0:
            yield at(st.comb_ready, small.next())
            slot, ps, free = small.take()
            wait(pe, st.comb_ready, free)
            for qt in range(QT):
                last = pe.transpose(ps[0:E0, qt * P:(qt + 1) * P], st.comb[:, qt, 0:E0], ident[:])
            st.comb_read = turned = c_pe.after(last)
            wait(act, turned, st.tmpT_read)
            copied = c_act.after(act.activation(st.tmpT[0:E0, :], ps[0:E0, 0:S], ACT.Copy))
            small.release(slot, copied)
            yield at(copied, small.next())
            slot, ps, free = small.take()
            wait(pe, copied, free)
            for qt in range(QT):
                last = pe.matmul(ps[:, qt * D:(qt + 1) * D], st.tmpT[0:E0, qt * P:(qt + 1) * P], b_eo[:],
                                 start=True, stop=True)
            st.tmpT_read = made = c_pe.after(last)
            wait(dve, made, residual_ready)
            flat = st.x[:].rearrange("p a d -> p (a d)")
            residual_ready = c_dve.after(dve.tensor_tensor(flat, ps[:, 0:QT * D], flat, ALU.add))
            small.release(slot, residual_ready)
        loads = []

        def load():
            eslot, weights, wfree = experts.take()
            wait(sp, wfree)
            loads.append((eslot, weights, c_expert[eslot].after(sp.dma_start(
                weights[:].rearrange("p a n -> p (a n)"), t["experts"][layer * E0 + load.e]))))
            load.e += 1

        load.e = 0

        def first(e):
            eslot, weights, loaded = loads.pop(0)
            slot, ps, free = scores.take()
            wait(pe, loaded, st.xT_ready, free)
            for f in range(NF):
                last = pe.matmul(ps[:, f, :], weights[:, 0, f * P:(f + 1) * P], st.xT[:], start=True, stop=True)
            st.xT_read = made = c_pe.after(last, 1.75)
            hslot, hid, hfree = hidden.take()
            wait(act, made, hfree)
            if layer == 0:
                for f in range(NF):
                    ready = c_act.after(act.activation(hid[:, f, :], ps[:, f, :], ACT.Gelu,
                                                       bias=b_hid[:, e, f:f + 1]), 0.36)
            else:
                ready = c_act.after(act.activation(hid[:], ps[:], ACT.Tanh, scale=0.5), 0.9)
                wait(dve, ready)
                ready = c_dve.after(dve.scalar_tensor_tensor(
                    out=hid[:].rearrange("p a b -> p (a b)"), in0=hid[:].rearrange("p a b -> p (a b)"), scalar=1.0,
                    in1=ps[:].rearrange("p a b -> p (a b)"), op0=ALU.add, op1=ALU.mult), 1.3)
            scores.release(slot, ready)
            return e, eslot, weights, hslot, hid, ready

        def second(e, eslot, weights, hslot, hid, ready):
            slot, ps, free = small.take()
            wait(pe, ready, free)
            for qt in range(QT):
                for f in range(NF):
                    last = pe.matmul(ps[:, qt * D:(qt + 1) * D], hid[:, f, qt * P:(qt + 1) * P],
                                     weights[:, 1, f * D:(f + 1) * D], start=f == 0, stop=f == NF - 1)
            made = c_pe.after(last, 1.8)
            hidden.release(hslot, made)
            experts.release(eslot, made)
            wait(dve, made, st.x_ready, residual_ready, st.comb_ready)
            for qt in range(QT):
                st.x_ready = c_dve.after(dve.scalar_tensor_tensor(
                    out=st.x[:, qt, :], in0=ps[:, qt * D:(qt + 1) * D], scalar=st.comb[:, qt, e:e + 1],
                    in1=st.x[:, qt, :], op0=ALU.mult, op1=ALU.add))
            small.release(slot, st.x_ready)

        before = None
        for e in range(count):
            if not loads:
                if before is not None:
                    yield at(before[-1], small.next())
                    second(*before)
                    before = None
                yield from until_free(experts)
                load()
            if load.e < count and experts.free:
                load()
            if not hidden.free and before is not None:
                yield at(before[-1], small.next())
                second(*before)
                before = None
            yield from until_free(hidden)
            yield at(loads[0][2], st.xT_ready, scores.next())
            if not hidden.free:
                yield from until_free(hidden)
            begun = first(e)
            if before is not None:
                yield at(before[-1], small.next())
                second(*before)
            before = begun
        yield at(before[-1], small.next())
        second(*before)
        st.comb_read = st.x_ready

    def first_layer(st, batch, prepare_context):
        b = bass.ds(batch, 1)
        loaded = st.c_x.after(sp.dma_start(st.x[:], t["x"][b].rearrange("a (q p) d -> (a p) q d", p=P)))
        yield from transpose_state(st, st.x, loaded)
        steps = [self_attention(st, 0, causal_q, causal_k, None, 0, st.xT_ready)]
        if prepare_context:
            steps.append(context(st, 0, batch))
        yield from alternate(*steps)
        yield from layer_norm(st, st.x_ready, 4, 5)
        yield from transpose_state(st, st.x, st.x_ready)
        yield from cross_attention(st, 0, None, None, None, 1, st.xT_ready)
        yield from layer_norm(st, st.x_ready, 6, 7)
        yield from transpose_state(st, st.x, st.x_ready)
        yield from route(st, 0, st.x_ready)
        yield from alternate(experts_of(st, 0, st.x_ready), context(st, 1, batch), masks(st, batch))

    def second_layer(st, batch, next_batch):
        yield from layer_norm(st, st.x_ready, 8, 9)
        yield from rms_norm(st, st.x_ready, 10)
        yield from transpose_state(st, st.tmp, st.normed)
        yield from self_attention(st, 1, st.mself_q, st.mself_k, st.mself_ready, 2, st.normed)
        yield from rms_norm(st, st.x_ready, 11)
        yield from transpose_state(st, st.tmp, st.normed)
        yield from cross_attention(st, 1, mask_bias_q, mask_bias_k, st.mcross_ready, 3, st.normed)
        cross_bias.release(0, st.keys_read)
        yield from rms_norm(st, st.x_ready, 12)
        yield from transpose_state(st, st.tmp, st.normed)
        yield from route(st, 1, st.normed)
        wait(dve, st.comb_read)
        st.comb_ready = c_dve.after(dve.memset(st.comb[:, :, E1:E1 + 1], 0.5))
        steps = [experts_of(st, 1, st.x_ready)]
        if next_batch is not None:
            steps.append(context(st, 0, next_batch))
        yield from alternate(*steps)
        yield at(st.x_ready)
        wait(sp, st.x_ready)
        stored = st.c_out.after(sp.dma_start(
            out[bass.ds(batch, 1)].rearrange("a (q p) d -> (a p) q d", p=P), st.x[:]))
        wait(sp, stored)

    def issue(*steps):
        for _ in alternate(*steps):
            pass

    odd, even = streams
    issue(first_layer(even, 0, True), context(odd, 0, 1))
    restart()
    with nc.Fori(0, PAIRS - 1) as i:
        issue(chain(first_layer(odd, i * 2 + 1, False), second_layer(odd, i * 2 + 1, i * 2 + 3)),
              chain(second_layer(even, i * 2, i * 2 + 2), first_layer(even, i * 2 + 2, False)))
        restart()
    issue(chain(first_layer(odd, B - 1, False), second_layer(odd, B - 1, None)), second_layer(even, B - 2, None))


def kernel(**inputs):
    import concourse.bacc as bacc
    from concourse.bass_utils import run_bass_kernel_spmd

    a = {k: np.asarray(v) for k, v in inputs.items()}
    f32 = np.float32

    def layer(n):
        return lambda name: a[f"L{n}_xattn_{name}"]

    l0, l1 = layer(0), layer(1)
    zero = np.zeros(D, f32)

    def values(w):
        padded = np.zeros((D, H, VW), f32)
        padded[:, :, :HD] = w.reshape(D, H, HD)
        return padded.reshape(D, VCOLS)

    def value_bias(b):
        padded = np.ones((H, VW), f32)
        padded[:, :HD] = b.reshape(H, HD)
        return np.broadcast_to(padded.reshape(1, VCOLS), (P, VCOLS))

    def thrice(w):
        return np.repeat(w.reshape(D, NG, 1, GR), 3, axis=2).reshape(D, NG, QROWS)

    def row_bias(b):
        return np.tile(b.reshape(NG, GR).T, (3, 1))

    tri = np.tril(np.ones((S, S), bool))
    causal = np.where(tri, f32(0), f32(-BIG)).astype(f32)

    def tiles(m):
        return m.reshape(QT, P, S).transpose(1, 0, 2)

    def expert(w1, w2):
        return np.concatenate([w1, w2.reshape(NF, P, D).transpose(1, 0, 2).reshape(P, NF * D)], axis=1)

    w1s = [l0("e_w1")[e] for e in range(E0)] + [l1("exp_w1")[e].T for e in range(E1)] + [l1("sh_w1").T]
    w2s = [l0("e_w2")[e] for e in range(E0)] + [l1("exp_w2")[e].T for e in range(E1)] + [l1("sh_w2").T]
    arrays = {
        "x": a["x"],
        "ctxT": a["ctx_1024"].transpose(0, 2, 1),
        "mself": a["mask_BxSxS_ik0"],
        "mselfT": a["mask_BxSxS_ik0"].transpose(0, 2, 1),
        "mcross": a["mask_BxSxS2_if1"],
        "mcrossT": a["mask_BxSxS2_if1"].transpose(0, 2, 1),
        "ident": np.eye(P, dtype=f32),
        "head_sel": np.tile(np.kron(np.eye(HG, dtype=f32), np.ones((HD, 1), f32)), (3, 1)),
        "iota": np.broadcast_to(np.arange(E0, dtype=f32), (P, E0)),
        "causal_q": tiles(causal),
        "causal_k": tiles(causal.T),
        "w_split": np.stack([
            np.stack([thrice(l0("sa_wq")), thrice(l0("sa_wk")), thrice(l0("ca_wq"))]),
            np.stack([thrice(l1("sa_wq").T), thrice(l1("sa_wk").T), thrice(l1("ca_wq").T)]),
        ]).transpose(2, 0, 1, 3, 4),
        "w_key": np.stack([l0("ca_wk"), l1("ca_wk").T], axis=1),
        "w_val": np.stack([np.stack([values(l0("sa_wv")), values(l0("ca_wv"))]),
                           np.stack([values(l1("sa_wv").T), values(l1("ca_wv").T)])]).transpose(2, 0, 1, 3),
        "w_out": np.stack([np.stack([l0("sa_wo"), l0("ca_wo")]),
                           np.stack([l1("sa_wo").T, l1("ca_wo").T])]).transpose(2, 0, 1, 3),
        "b_q": np.stack([np.stack([row_bias(l0("sa_bq")), row_bias(l0("sa_bk")), row_bias(l0("ca_bq"))]),
                         np.stack([row_bias(zero)] * 3)]).transpose(2, 0, 1, 3),
        "b_k": np.stack([l0("ca_bk"), zero], axis=1),
        "b_val": np.stack([np.stack([value_bias(l0("sa_bv")), value_bias(l0("ca_bv"))]),
                           np.stack([value_bias(zero)] * 2)]).transpose(2, 0, 1, 3),
        "rows": np.broadcast_to(np.stack([
            l0("sa_bo"), l0("ca_bo"), zero, zero, l0("ln1_g"), l0("ln1_b"), l0("ln2_g"), l0("ln2_b"), l0("ln3_g"),
            l0("ln3_b"), l1("norm1_w"), l1("norm2_w"), l1("norm3_w")]), (P, 13, D)),
        "router": np.stack([l0("router_w"), l1("gate_w").T], axis=1),
        "router_b": np.broadcast_to(l0("router_b"), (P, E0)),
        "b_hid": l0("e_b1").reshape(E0, NF, P).transpose(2, 0, 1),
        "b_eo": l0("e_b2"),
        "halves": np.full((P, 2), -0.5, f32),
        "experts": np.stack([expert(w1, w2) for w1, w2 in zip(w1s, w2s)]),
    }
    arrays = {k: np.ascontiguousarray(v) for k, v in arrays.items()}
    nc = bacc.Bacc("TRN2", target_bir_lowering=False, num_devices=1, dynamic_dma_scratch_size=1024)
    t = {k: nc.dram_tensor(f"in_{k}", v.shape, mybir.dt.from_np(v.dtype), kind="ExternalInput").ap()
         for k, v in arrays.items()}
    out = nc.dram_tensor("out_x", (B, S, D), F32, kind="ExternalOutput").ap()
    build(nc, t, out)
    r = run_bass_kernel_spmd(nc, [{f"in_{k}": v for k, v in arrays.items()}], core_ids=[0])
    return r.results[0]["out_x"]
```

```python
from contextlib import ExitStack

import numpy as np

import concourse.bass as bass
from concourse import mybir

F32 = mybir.dt.float32
F32R = mybir.dt.float32r
BF16 = mybir.dt.bfloat16
I32 = mybir.dt.int32
U32 = mybir.dt.uint32
ALU = mybir.AluOpType
ACT = mybir.ActivationFunctionType
AX = mybir.AxisListType.X

B, S, D, SK = 16, 256, 128, 1601
H, HD = 16, 8
P = 128
QT = S // P
HG = 4
NG = H // HG
GR = HG * HD
QROWS = 3 * GR
MROW = QROWS
KROWS = QROWS + 1
VW = HD + 1
VCOLS = H * VW
VPAD = 32 - VW
CHUNK = 402
E0, E1, FF, TOPK = 8, 8, 512, 2
NF = FF // P
EPS = 1e-5
BIG = 2.0 ** 100
LAG = dict(maxima=0.0, scores=-1.0, weigh=0.0, first=0.0, second=-1.0, context=0.0, masks=0.0, queries=0.0, odd=0.0)
SCALE = float(1.0 / np.sqrt(np.float32(HD)))
PAIRS = B // 2


def spans(n, step):
    return [(a, min(step, n - a)) for a in range(0, n, step)]


class Counter:

    def __init__(self, ctx, nc, name, clock, engine, step=1, usual=0.2, latency=0.1):
        self.sem, self.step, self.value = ctx.enter_context(nc.semaphore(name)), step, 0
        self.clock, self.engine, self.usual, self.latency = clock, id(engine), usual, latency

    def after(self, instruction, us=None):
        instruction.then_inc(self.sem, self.step)
        self.value += self.step
        self.clock[self.engine] += self.usual if us is None else us
        return (self, self.value, self.clock[self.engine] + self.latency)


class Ring:

    def __init__(self, buffers):
        self.buffers = buffers
        self.restart()

    def restart(self):
        self.free = [(n, None) for n in range(len(self.buffers))]

    def take(self):
        slot, mark = self.free.pop(0)
        return slot, self.buffers[slot], mark

    def release(self, slot, mark):
        self.free.append((slot, mark))

    def next(self):
        return self.free[0][1] if self.free else None


def at(*marks):
    return max((mark[2] for mark in marks if mark is not None), default=0.0)


def alternate(*streams):
    ready = [0.0] * len(streams)
    live = list(range(len(streams)))
    while live:
        k = min(live, key=lambda n: ready[n])
        try:
            ready[k] = next(streams[k])
        except StopIteration:
            live.remove(k)
            continue
        yield min(ready[n] for n in live)


def chain(*steps):
    for one in steps:
        yield from one


def later(lag, *steps):
    for ready in chain(*steps):
        yield ready + lag


def build(nc, t, out):
    with ExitStack() as ctx:
        program(ctx, nc, t, out)


def program(ctx, nc, t, out):
    pe, dve, act, pool, sp = nc.tensor, nc.vector, nc.scalar, nc.gpsimd, nc.sync

    def sb(name, shape, dtype=F32):
        return ctx.enter_context(nc.sbuf_tensor(name, shape, dtype))

    ident = sb("ident", [P, P])
    ident_b = sb("ident_b", [P, P], BF16)
    head_sel = sb("head_sel", [QROWS, HG])
    iota = sb("iota", [P, E0])
    causal_q = sb("causal_q", [P, QT, S], BF16)
    causal_k = sb("causal_k", [P, QT, S], BF16)
    w_split = sb("w_split", [P, 2, 3, NG, QROWS])
    w_key = sb("w_key", [P, 2, D])
    w_val = sb("w_val", [P, 2, 2, VCOLS])
    w_out = sb("w_out", [P, 2, 2, D])
    b_q = sb("b_q", [QROWS, 2, 3, NG])
    b_k = sb("b_k", [P, 2])
    b_val = sb("b_val", [P, 2, 2, VCOLS])
    rows = sb("rows", [P, 11, D])
    router = sb("router", [P, 2, E0])
    router_b = sb("router_b", [P, E0])
    b_hid = sb("b_hid", [P, E0, NF])
    b_eo = sb("b_eo", [E0, D])
    halves = sb("halves", [P, 2])

    context_in = Ring([sb("ctxT", [P, SK])])
    split_keys = Ring([(sb("k_hi", [P, SK], F32R), sb("k_lo", [P, SK], F32R))])
    mask_words = Ring([sb("mask_words", [P, SK], I32)])
    probs = Ring([sb(f"probs{n}", [P, HG, S]) for n in range(3)])
    hidden = Ring([sb(f"hidden{n}", [P, NF, S]) for n in range(2)])
    q_diag = Ring([sb(f"q_diag{n}", [KROWS, HG, S], F32R) for n in range(3)])
    experts = Ring([sb(f"expert{n}", [P, 2, FF]) for n in range(3)])
    neg_max_row = Ring([sb(f"neg_max_row{n}", [HG, S], F32R) for n in range(3)])
    mask_bias_q, mask_bias_k = sb("mask_bias_q", [P, QT, SK], BF16), sb("mask_bias_k", [P, 13, S], BF16)
    cross_bias = Ring([(mask_bias_q, mask_bias_k)])

    scores = Ring([ctx.enter_context(nc.psum_tensor(f"scores{n}", [P, HG, S], F32)) for n in range(2)])
    small = Ring([ctx.enter_context(nc.psum_tensor(f"small{n}", [P, 512], F32)) for n in range(3)])
    sums = Ring([ctx.enter_context(nc.psum_tensor(f"sums{n}", [P, 512], F32)) for n in range(1)])

    clock = {id(engine): 0.0 for engine in (pe, dve, act, pool, sp)}
    c_pe = Counter(ctx, nc, "c_pe", clock, pe, usual=0.3)
    c_dve = Counter(ctx, nc, "c_dve", clock, dve)
    c_act = Counter(ctx, nc, "c_act", clock, act, usual=0.26)
    c_pool = Counter(ctx, nc, "c_pool", clock, pool, usual=0.5)
    counters = [c_pe, c_dve, c_act, c_pool]

    def dma_counter(name, engine=sp, latency=2.5):
        c = Counter(ctx, nc, name, clock, engine, 16, usual=0.05, latency=latency)
        counters.append(c)
        return c

    c_ctx, c_mask, c_setup = dma_counter("c_ctx", latency=7.0), dma_counter("c_mask", latency=7.0), dma_counter("c_setup")
    c_expert = [dma_counter(f"c_expert{n}", latency=5.0) for n in range(len(experts.buffers))]
    c_maxrow = [dma_counter(f"c_maxrow{n}", act) for n in range(len(q_diag.buffers))]
    reached = {}

    def wait(engine, *marks):
        for mark in marks:
            if mark is None:
                continue
            counter, value, time = mark
            key = (id(engine), id(counter))
            if reached.get(key, 0) < value:
                engine.wait_ge(counter.sem, value)
                reached[key] = value
            clock[id(engine)] = max(clock[id(engine)], time)

    w_loads = [(ident, "ident"), (head_sel, "head_sel"), (iota, "iota"), (w_split, "w_split"), (w_key, "w_key"), (w_val, "w_val"),
               (w_out, "w_out"), (b_q, "b_q"), (b_k, "b_k"), (b_val, "b_val"), (rows, "rows"),
               (router, "router"), (router_b, "router_b"), (b_hid, "b_hid"), (b_eo, "b_eo"), (halves, "halves")]
    for n, (tile, name) in enumerate(w_loads):
        loaded = c_setup.after((sp, act)[n % 2].dma_start(tile[:], t[name]))
    for n, name in enumerate(("causal_q", "causal_k")):
        loaded = c_setup.after(sp.dma_start(probs.buffers[n][:, 0:QT, :], t[name]))
    wait(dve, loaded)
    c_dve.after(dve.tensor_copy(causal_q[:], probs.buffers[0][:, 0:QT, :]))
    c_dve.after(dve.tensor_copy(causal_k[:], probs.buffers[1][:, 0:QT, :]))
    c_dve.after(dve.tensor_copy(ident_b[:], ident[:]))

    class Stream:

        def __init__(self, n):
            self.n = n
            self.x = sb(f"x{n}", [P, QT, D])
            self.x_in = sb(f"x_in{n}", [P, QT, D])
            self.xT = sb(f"xT{n}", [P, S])
            self.q = sb(f"q{n}", [QROWS, NG, S], F32R)
            self.ks = sb(f"ks{n}", [KROWS, NG, S], F32R)
            self.vs = sb(f"vs{n}", [P, QT * VCOLS + VPAD])
            self.kc = sb(f"kc{n}", [KROWS, NG, SK], F32R)
            self.vc = sb(f"vc{n}", [P, 13 * VCOLS + VPAD])
            self.o = sb(f"o{n}", [P, NG, S])
            self.tmp = sb(f"tmp{n}", [P, QT, D])
            self.tmpT = sb(f"tmpT{n}", [P, S])
            self.chunk_max = sb(f"chunk_max{n}", [P, QT * HG, 4])
            self.neg_max = sb(f"neg_max{n}", [P, QT * HG])
            self.stats = sb(f"stats{n}", [P, QT, 6])
            self.mean_var = sb(f"mean_var{n}", [P, QT, 2])
            self.rstd = sb(f"rstd{n}", [P, QT])
            self.rden = sb(f"rden{n}", [P, QT, H])
            self.lg = sb(f"lg{n}", [P, QT, E0])
            self.top = sb(f"top{n}", [P, QT, 8])
            self.idx = sb(f"idx{n}", [P, QT, 8], U32)
            self.idxf = sb(f"idxf{n}", [P, QT, 8])
            self.gate = sb(f"gate{n}", [P, QT, 4])
            self.pick = sb(f"pick{n}", [P, QT, E0])
            self.comb = sb(f"comb{n}", [P, QT, E0 + 1])
            self.mself_q = sb(f"mself_q{n}", [P, QT, S], BF16)
            self.mself_k = sb(f"mself_k{n}", [P, QT, S], BF16)
            self.c_x = dma_counter(f"c_x{n}")
            self.c_kc = dma_counter(f"c_kc{n}", latency=8.0)
            self.c_out = dma_counter(f"c_out{n}")
            self.restart()

        def restart(self):
            self.stored = self.x_loaded = self.x_in_read = None
            self.xT_read = self.ks_read = self.vs_read = self.kc_read = self.vc_read = self.q_read = None
            self.neg_max_read = self.o_read = self.tmp_read = self.tmpT_read = self.comb_read = None
            self.x_ready = self.xT_ready = self.comb_ready = self.kc_ready = self.vc_ready = None
            self.mself_ready = self.mcross_ready = self.mself_read = None
            self.group = {}
            self.loads, self.loaded = 0, []

    streams = [Stream(0), Stream(1)]
    for st in streams:
        c_dve.after(dve.memset(st.ks[MROW:KROWS].bitcast(F32), 1.0))
        c_pool.after(pool.memset(st.kc[MROW:KROWS].bitcast(F32), 1.0))
        c_dve.after(dve.memset(st.vs[:, QT * VCOLS:], 0.0))
        c_dve.after(dve.memset(st.vc[:, 12 * VCOLS:], 0.0))

    def restart():
        for st in streams:
            wait(sp, st.stored)
        nc.all_engine_barrier()
        for n, c in enumerate(counters):
            (sp, pool, act, dve)[n % 4].sem_clear(c.sem)
            c.value = 0
        nc.all_engine_barrier()
        reached.clear()
        for ring in (probs, hidden, q_diag, experts, neg_max_row, scores, small, sums, context_in, split_keys,
                     mask_words):
            ring.restart()
        for st in streams:
            st.restart()
        for engine in clock:
            clock[engine] = 0.0

    restart()

    def until_free(ring):
        later = 0.0
        while not ring.free:
            later = max(later, clock[id(pe)]) + 0.5
            yield later

    def transpose_state(st, source, ready):
        yield at(ready, small.next())
        slot, ps, free = small.take()
        wait(pe, ready, free)
        for qt in range(QT):
            last = pe.transpose(ps[:, qt * P:(qt + 1) * P], source[:, qt, :], ident[:])
        st.tmp_read = turned = c_pe.after(last, 0.45)
        wait(act, turned, st.xT_read)
        st.xT_ready = c_act.after(act.activation(st.xT[:], ps[:, 0:S], ACT.Copy), 0.36)
        small.release(slot, st.xT_ready)

    def inverse_root(st, ready):
        wait(pool, ready)
        return c_pool.after(pool.tensor_tensor(st.rstd[:], st.mean_var[:, :, 1], halves[:], ALU.pow), 0.63)

    def layer_norm(st, ready, gain, bias):
        wait(dve, ready)
        for qt in range(QT):
            done = c_dve.after(dve.bn_stats(st.stats[:, qt, :], st.x[:, qt, :]))
        wait(dve, done)
        for qt in range(QT):
            done = c_dve.after(dve.bn_aggr(st.mean_var[:, qt, :], st.stats[:, qt, :]))
        wait(dve, done)
        done = c_dve.after(dve.tensor_scalar(st.mean_var[:, :, 1], st.mean_var[:, :, 1], EPS, None, ALU.add))
        rooted = inverse_root(st, done)
        yield at(rooted)
        wait(dve, rooted)
        for qt in range(QT):
            done = c_dve.after(dve.tensor_scalar(st.x[:, qt, :], st.x[:, qt, :], st.mean_var[:, qt, 0:1],
                                                 st.rstd[:, qt:qt + 1], ALU.subtract, ALU.mult))
        wait(dve, done)
        done = c_dve.after(dve.tensor_tensor(st.x[:], st.x[:], wide(rows[:, gain, :], QT), ALU.mult))
        wait(dve, done)
        st.x_ready = c_dve.after(dve.tensor_tensor(st.x[:], st.x[:], wide(rows[:, bias, :], QT), ALU.add), 0.3)

    def wide(ap, n):
        return ap.unsqueeze(1).to_broadcast([ap.shape[0], n, ap.shape[1]])

    def rms_norm(st, ready, gain):
        wait(dve, ready, st.tmp_read)
        for qt in range(QT):
            done = c_dve.after(dve.tensor_tensor_reduce(st.tmp[:, qt, :], st.x[:, qt, :], st.x[:, qt, :], 1.0 / D,
                                                        EPS, ALU.mult, ALU.add, st.mean_var[:, qt, 1:2]))
        rooted = inverse_root(st, done)
        yield at(rooted)
        wait(dve, rooted)
        for qt in range(QT):
            done = c_dve.after(dve.scalar_tensor_tensor(
                out=st.tmp[:, qt, :], in0=st.x[:, qt, :], scalar=st.rstd[:, qt:qt + 1], in1=rows[:, gain, :],
                op0=ALU.mult, op1=ALU.mult))
        st.normed = done

    def project_split(st, weight, bias, dest, lo_rows, dest_free):
        slot, ps, free = scores.take()
        wait(pe, st.xT_ready, free)
        made = []
        for g in range(NG):
            made.append(c_pe.after(pe.matmul(ps[0:QROWS, g, :], weight[:, g, :], st.xT[:], start=True, stop=True),
                                   0.34))
        st.xT_read = made[-1]
        wait(dve, *dest_free)
        a, b = lo_rows
        high, done = [], []
        for g in range(NG + 1):
            if g < NG:
                wait(dve, made[g // 2 * 2 + 1])
                high.append(c_dve.after(dve.tensor_scalar(dest[0:QROWS, g, :], ps[0:QROWS, g, :],
                                                          bias[:, g:g + 1], None, ALU.add), 0.39))
            if g > 0:
                wait(dve, high[g - 1])
                done.append(c_dve.after(dve.scalar_tensor_tensor(
                    out=dest[a:b, g - 1, :], in0=ps[a:b, g - 1, :], scalar=bias[a:b, g - 1:g],
                    in1=dest[a:b, g - 1, :].bitcast(F32), op0=ALU.add, op1=ALU.subtract), 0.39))
        scores.release(slot, done[-1])
        return done

    def self_values(st, layer):
        slot, ps, free = small.take()
        wait(pe, st.xT_ready, free)
        for kt in range(QT):
            last = pe.matmul(ps[:, kt * VCOLS:(kt + 1) * VCOLS], st.xT[:, kt * P:(kt + 1) * P],
                             w_val[:, layer, 0, :], start=True, stop=True)
        st.xT_read = made = c_pe.after(last, 0.24)
        wait(dve, made, st.vs_read)
        n = QT * VCOLS
        done = c_dve.after(dve.tensor_tensor(st.vs[:, 0:n].rearrange("p (k v) -> p k v", k=QT),
                                             ps[:, 0:n].rearrange("p (k v) -> p k v", k=QT),
                                             wide(b_val[:, layer, 0, :], QT), ALU.add), 0.4)
        small.release(slot, done)
        return done

    def maxima(st, g, keys, keys_ready, n_keys, mask, mask_ready, causal):
        yield from until_free(q_diag)
        slot, qd, free = q_diag.take()
        yield at(st.q_ready[g], free) + LAG["queries"]
        wait(pool, st.q_ready[g], free)
        for j in range(HG):
            built = c_pool.after(pool.tensor_scalar(qd[0:QROWS, j, :], st.q[:, g, :].bitcast(F32),
                                                    head_sel[:, j:j + 1], 1.0, ALU.mult, ALU.mult), 0.46)
        if g == NG - 1:
            st.q_read = built
        parts = [(min(k0, max(n_keys - CHUNK, 0)), min(CHUNK, n_keys)) for k0, _ in spans(n_keys, CHUNK)]
        for qt in range(QT):
            for j in range(HG):
                for c, (k0, kn) in enumerate([(0, (qt + 1) * P)] if causal else parts):
                    yield at(built, keys_ready[g], small.next()) + LAG["maxima"]
                    pslot, ps, pfree = small.take()
                    wait(pe, built, keys_ready[g], pfree)
                    made = c_pe.after(pe.matmul(ps[:, 0:kn], qd[0:QROWS, j, qt * P:(qt + 1) * P],
                                                keys[0:QROWS, g, k0:k0 + kn], start=True, stop=True), 0.5 * kn / 1000)
                    wait(dve, made, mask_ready, st.neg_max_read)
                    result = st.chunk_max[:, qt * HG + j, c:c + 1]
                    if mask is None:
                        done = dve.tensor_reduce(result, ps[:, 0:kn], AX, ALU.max)
                    else:
                        done = dve.tensor_tensor_reduce(ps[:, 0:kn], ps[:, 0:kn], mask[:, qt, k0:k0 + kn], 1.0,
                                                        -3e38, ALU.add, ALU.max, result)
                    done = c_dve.after(done, 0.08 + kn / 960)
                    small.release(pslot, done)
        wait(dve, done)
        negated = c_dve.after(dve.tensor_reduce(st.neg_max[:], st.chunk_max[:, :, 0:len(parts)], AX, ALU.max,
                                                negate=True))
        yield at(negated, small.next())
        pslot, ps, pfree = small.take()
        wait(pe, negated, pfree)
        for qt in range(QT):
            last = pe.transpose(ps[0:HG, qt * P:(qt + 1) * P], st.neg_max[:, qt * HG:(qt + 1) * HG], ident[:])
        st.neg_max_read = turned = c_pe.after(last)
        rslot, row, rfree = neg_max_row.take()
        wait(act, turned, rfree)
        copied = c_act.after(act.activation(row[:], ps[0:HG, 0:S], ACT.Copy))
        small.release(pslot, copied)
        wait(act, copied)
        placed = c_maxrow[slot].after(act.dma_start(qd[MROW:KROWS, :, :].bitcast(F32), row[:].bitcast(F32)))
        neg_max_row.release(rslot, placed)
        st.group[g] = (slot, qd, placed)

    def exponentials(st, g, keys, n_keys, values, values_ready, mask, causal):
        slot, qd, placed = st.group[g]
        yield from until_free(sums)
        oslot, acc, ofree = sums.take()
        parts = spans(n_keys, P)
        waiting = []

        def weigh():
            kt, kn, seen, pslot, pr, expd = waiting.pop(0)
            wait(pe, expd)
            if kt == 0:
                wait(pe, ofree, values_ready)
            for j in range(HG):
                v0 = kt * VCOLS + (g * HG + j) * VW
                last = pe.matmul(acc[32 * j:32 * j + 32, seen], values[0:kn, v0:v0 + 32], pr[0:kn, j, seen],
                                 start=kt == 0, stop=kt == len(parts) - 1)
            st.summed = c_pe.after(last, 0.52)
            probs.release(pslot, st.summed)

        for kt, (k0, kn) in enumerate(parts):
            yield at(placed, scores.next()) + LAG["scores"]
            seen = slice(kt * P if causal else 0, S)
            sslot, ps, sfree = scores.take()
            wait(pe, placed, sfree)
            for half in range(2):
                pair = slice(2 * half, 2 * half + 2)
                last = pe.matmul(ps[0:kn, pair, seen], keys[:, g, k0:k0 + kn], qd[:, pair, seen], start=True,
                                 stop=mask is None)
                if mask is not None:
                    biased = slice(kt * P, (kt + 1) * P) if causal else seen
                    last = pe.matmul(ps[0:kn, pair, biased], ident_b[0:kn, 0:kn], wide(mask[0:kn, kt, biased], 2),
                                     start=False, stop=True)
            st.keys_read = made = c_pe.after(last, 0.48 if mask is None else 0.92)
            pslot, pr, pfree = probs.take()
            wait(act, made, pfree)
            expd = c_act.after(act.activation(pr[0:kn, :, seen], ps[0:kn, :, seen], ACT.Exp, scale=SCALE), 0.9)
            scores.release(sslot, expd)
            waiting.append((kt, kn, seen, pslot, pr, expd))
            if len(waiting) > 1:
                yield at(waiting[0][5], ofree, values_ready) + LAG["weigh"]
                weigh()
        q_diag.release(slot, st.keys_read)
        yield at(expd, ofree, values_ready)
        weigh()
        wait(act, st.summed, st.o_read)
        st.o_ready = c_act.after(act.activation(st.o[:, g, :], acc[:, 0:S], ACT.Copy))
        sums.release(oslot, st.o_ready)

    def attention(st, layer, cross, keys, keys_ready, n_keys, values, values_ready, mask_q, mask_k, mask_ready,
                  bias_row, residual_ready, residual):
        causal = layer == 0 and not cross
        if bias_row is not None:
            wait(pool, residual_ready, st.stored)
            st.x_ready = c_pool.after(pool.tensor_tensor(st.x[:], residual[:], wide(rows[:, bias_row, :], QT),
                                                         ALU.add), 0.7)
        if residual is st.x_in:
            st.x_in_read = st.x_ready
        yield from maxima(st, 0, keys, keys_ready, n_keys, mask_q, mask_ready, causal)
        wait(pe, mask_ready)
        for g in range(NG):
            steps = [exponentials(st, g, keys, n_keys, values, values_ready, mask_k, causal)]
            if g + 1 < NG:
                steps.append(maxima(st, g + 1, keys, keys_ready, n_keys, mask_q, mask_ready, causal))
            yield from alternate(*steps)
        st.values_read = st.summed
        for _ in range(2):
            if cross and experts.free:
                load_expert(st, layer)
        for qt in range(QT):
            yield at(st.o_ready, small.next())
            slot, ps, free = small.take()
            wait(pe, st.o_ready, free)
            for g in range(NG):
                last = pe.transpose(ps[:, g * P:(g + 1) * P], st.o[:, g, qt * P:(qt + 1) * P], ident[:])
            st.o_read = turned = c_pe.after(last, 0.45)
            by_head = ps[:].rearrange("p (h c) -> p h c", h=H)
            wait(dve, turned, st.tmp_read)
            inverted = c_dve.after(dve.reciprocal(st.rden[:, qt, :], by_head[:, :, HD]))
            wait(dve, inverted)
            done = c_dve.after(dve.tensor_tensor(
                st.tmp[:, qt, :].rearrange("p (h c) -> p h c", h=H), by_head[:, :, 0:HD],
                st.rden[:, qt, :].unsqueeze(2).to_broadcast([P, H, HD]), ALU.mult))
            small.release(slot, done)
        yield at(done, small.next())
        slot, ps, free = small.take()
        wait(pe, done, free)
        for qt in range(QT):
            last = pe.transpose(ps[:, qt * P:(qt + 1) * P], st.tmp[:, qt, :], ident[:])
        st.tmp_read = turned = c_pe.after(last)
        wait(act, turned, st.tmpT_read)
        copied = c_act.after(act.activation(st.tmpT[:], ps[:, 0:S], ACT.Copy))
        small.release(slot, copied)
        yield at(copied, small.next())
        slot, ps, free = small.take()
        wait(pe, copied, free)
        for qt in range(QT):
            last = pe.matmul(ps[:, qt * D:(qt + 1) * D], st.tmpT[:, qt * P:(qt + 1) * P],
                             w_out[:, layer, int(cross), :], start=True, stop=True)
        st.tmpT_read = made = c_pe.after(last)
        wait(dve, made, st.x_ready)
        st.x_ready = c_dve.after(dve.tensor_tensor(st.x[:].rearrange("p a d -> p (a d)"), ps[:, 0:QT * D],
                                                   st.x[:].rearrange("p a d -> p (a d)"), ALU.add))
        small.release(slot, st.x_ready)

    def self_attention(st, layer, mask_q, mask_k, mask_ready, bias_row, residual_ready, residual):
        yield at(st.xT_ready, scores.next())
        st.q_ready = project_split(st, w_split[:, layer, 0], b_q[:, layer, 0, :], st.q, (2 * GR, 3 * GR),
                                   [st.q_read])
        yield at(scores.next())
        k_done = project_split(st, w_split[:, layer, 1], b_q[:, layer, 1, :], st.ks, (GR, 2 * GR), [st.ks_read])
        v_done = self_values(st, layer)
        yield from attention(st, layer, False, st.ks, k_done, S, st.vs, v_done, mask_q, mask_k, mask_ready,
                             bias_row, residual_ready, residual)
        st.ks_read = st.keys_read
        st.vs_read = st.values_read

    def cross_attention(st, layer, mask_q, mask_k, mask_ready, bias_row, residual_ready):
        yield at(st.xT_ready, scores.next())
        st.q_ready = project_split(st, w_split[:, layer, 2], b_q[:, layer, 2, :], st.q, (2 * GR, 3 * GR),
                                   [st.q_read])
        yield from attention(st, layer, True, st.kc, [st.kc_ready] * NG, SK, st.vc, st.vc_ready, mask_q, mask_k,
                             mask_ready, bias_row, residual_ready, st.x)
        st.kc_read = st.keys_read
        st.vc_read = st.values_read

    def context(st, layer, batch):
        yield from until_free(context_in)
        cslot, ctxT, cfree = context_in.take()
        wait(sp, cfree)
        loaded = c_ctx.after(sp.dma_start(ctxT[:], t["ctxT"][bass.ds(batch, 1)].rearrange("a p n -> (a p) n")))
        yield from until_free(split_keys)
        kslot, (k_hi, k_lo), kfree = split_keys.take()
        for k0, kn in spans(SK, CHUNK):
            yield at(loaded, kfree, small.next()) + LAG["context"]
            slot, ps, free = small.take()
            wait(pe, loaded, free)
            made = c_pe.after(pe.matmul(ps[:, 0:kn], w_key[:, layer, :], ctxT[:, k0:k0 + kn], start=True,
                                        stop=True), 0.4)
            wait(dve, made, kfree)
            high = c_dve.after(dve.tensor_scalar(k_hi[:, k0:k0 + kn], ps[:, 0:kn], b_k[:, layer:layer + 1], None,
                                                 ALU.add), 0.5)
            wait(dve, high)
            low = c_dve.after(dve.scalar_tensor_tensor(
                out=k_lo[:, k0:k0 + kn], in0=ps[:, 0:kn], scalar=b_k[:, layer:layer + 1],
                in1=k_hi[:, k0:k0 + kn].bitcast(F32), op0=ALU.add, op1=ALU.subtract), 0.55)
            small.release(slot, low)
        yield at(low, st.kc_read)
        wait(sp, low, st.kc_read)
        for g in range(NG):
            yield at(st.kc_ready) - 6.5
            for part, source in enumerate((k_hi, k_lo, k_hi)):
                st.kc_ready = st.c_kc.after(sp.dma_start(st.kc[part * GR:(part + 1) * GR, g, :].bitcast(F32),
                                                         source[g * GR:(g + 1) * GR, :].bitcast(F32)))
        split_keys.release(kslot, st.kc_ready)
        tiles = spans(SK, P)
        for first in range(0, len(tiles), 3):
            some = tiles[first:first + 3]
            kn = some[0][1]
            yield at(loaded, small.next()) + LAG["context"]
            slot, ps, free = small.take()
            wait(pe, loaded, free)
            for n, (k0, _) in enumerate(some):
                last = pe.matmul(ps[0:kn, n * VCOLS:(n + 1) * VCOLS], ctxT[:, k0:k0 + kn], w_val[:, layer, 1, :],
                                 start=True, stop=True)
            made = c_pe.after(last, 0.39)
            wait(dve, made, st.vc_read)
            w = len(some)
            st.vc_ready = c_dve.after(dve.tensor_tensor(
                st.vc[0:kn, first * VCOLS:(first + w) * VCOLS].rearrange("p (k v) -> p k v", k=w),
                ps[0:kn, 0:w * VCOLS].rearrange("p (k v) -> p k v", k=w),
                wide(b_val[0:kn, layer, 1, :], w), ALU.add), 0.55)
            small.release(slot, st.vc_ready)
        context_in.release(cslot, made)

    def mask_bias(st, source, dest, dest_free):
        k, n = dest.shape[0], dest.shape[1] * dest.shape[2]
        yield from until_free(mask_words)
        slot, words, free = mask_words.take()
        view = words[0:k, 0:n].rearrange("p (a b) -> p a b", a=dest.shape[1])
        wait(sp, free)
        loaded = c_mask.after(sp.dma_start(view, source))
        yield at(loaded) + LAG["masks"]
        wait(dve, loaded, dest_free)
        done = c_dve.after(dve.tensor_scalar(dest, view, 0, -BIG, ALU.is_equal, ALU.mult), 0.63)
        mask_words.release(slot, done)
        st.masked = done

    def masks(st, batch):
        b = bass.ds(batch, 1)
        yield from mask_bias(st, t["mself"][b].rearrange("a (q p) k -> (a p) q k", p=P), st.mself_q[:],
                  st.mself_read)
        yield from mask_bias(st, t["mselfT"][b].rearrange("a (q p) k -> (a p) q k", p=P), st.mself_k[:],
                                   None)
        st.mself_ready = st.masked
        yield from until_free(cross_bias)
        _, _, masks_read = cross_bias.take()
        for qt in range(QT):
            yield at(masks_read)
            yield from mask_bias(st, t["mcross"][b, qt * P:(qt + 1) * P, :].rearrange("a p k -> p a k"),
                      mask_bias_q[:, qt:qt + 1, :], masks_read)
        full = SK // P
        for k0, kn in spans(full, 6):
            yield from mask_bias(st, t["mcrossT"][b, k0 * P:(k0 + kn) * P, :].rearrange("a (q p) k -> (a p) q k", p=P),
                      mask_bias_k[:, k0:k0 + kn, :], None)
        yield from mask_bias(st, t["mcrossT"][b, full * P:SK, :].rearrange("a p k -> p a k"),
                                    mask_bias_k[0:SK - full * P, full:full + 1, :], None)
        st.mcross_ready = st.masked

    def route(st, layer, ready):
        yield at(st.xT_ready, small.next())
        slot, ps, free = small.take()
        wait(pe, st.xT_ready, free)
        for qt in range(QT):
            last = pe.matmul(ps[:, qt * E0:(qt + 1) * E0], st.xT[:, qt * P:(qt + 1) * P], router[:, layer, :],
                             start=True, stop=True)
        made = c_pe.after(last)
        wait(dve, made)
        logits = ps[:, 0:QT * E0].rearrange("p (q e) -> p q e", q=QT)
        if layer == 0:
            done = c_dve.after(dve.tensor_tensor(st.lg[:], logits, wide(router_b[:], QT), ALU.add))
        else:
            done = c_dve.after(dve.tensor_copy(st.lg[:], logits))
        small.release(slot, done)
        if layer == 0:
            wait(dve, done)
            done = c_dve.after(dve.tensor_reduce(st.gate[:, :, 0], st.lg[:], AX, ALU.max))
            wait(dve, done)
            done = c_dve.after(dve.tensor_tensor(st.lg[:], st.lg[:],
                                                 st.gate[:, :, 0:1].to_broadcast([P, QT, E0]), ALU.subtract))
            wait(act, done)
            done = c_act.after(act.activation(st.lg[:], st.lg[:], ACT.Exp))
            yield at(done)
            wait(dve, done)
            done = c_dve.after(dve.tensor_reduce(st.gate[:, :, 0], st.lg[:], AX, ALU.add))
            wait(dve, done)
            done = c_dve.after(dve.reciprocal(st.gate[:, :, 1], st.gate[:, :, 0]))
            wait(dve, done)
            done = c_dve.after(dve.tensor_tensor(st.lg[:], st.lg[:],
                                                 st.gate[:, :, 1:2].to_broadcast([P, QT, E0]), ALU.mult))
        wait(dve, done)
        for qt in range(QT):
            done = c_dve.after(dve.max(st.top[:, qt, :], st.lg[:, qt, :]))
        wait(dve, done)
        for qt in range(QT):
            done = c_dve.after(dve.max_index(st.idx[:, qt, :], st.top[:, qt, :], st.lg[:, qt, :]))
        found = done
        done = c_dve.after(dve.tensor_tensor(st.gate[:, :, 2], st.top[:, :, 1], st.top[:, :, 0], ALU.subtract))
        wait(act, done)
        done = c_act.after(act.activation(st.gate[:, :, 2], st.gate[:, :, 2], ACT.Exp))
        wait(dve, found)
        turned = c_dve.after(dve.tensor_copy(st.idxf[:], st.idx[:]))
        yield at(done)
        wait(dve, done)
        done = c_dve.after(dve.tensor_scalar(st.gate[:, :, 3], st.gate[:, :, 2], 1.0, None, ALU.add))
        wait(dve, done)
        done = c_dve.after(dve.reciprocal(st.gate[:, :, 0], st.gate[:, :, 3]))
        wait(dve, done)
        if layer == 1:
            done = c_dve.after(dve.tensor_scalar(st.gate[:, :, 0], st.gate[:, :, 0], 0.5, None, ALU.mult))
            wait(dve, done)
        done = c_dve.after(dve.tensor_tensor(st.gate[:, :, 1], st.gate[:, :, 0], st.gate[:, :, 2], ALU.mult))
        wait(dve, done, turned, st.comb_read)
        for qt in range(QT):
            done = c_dve.after(dve.tensor_scalar(st.pick[:, qt, :], iota[:], st.idxf[:, qt, 0:1],
                                                 st.gate[:, qt, 0:1], ALU.is_equal, ALU.mult))
            done = c_dve.after(dve.tensor_scalar(st.comb[:, qt, 0:E0], iota[:], st.idxf[:, qt, 1:2],
                                                 st.gate[:, qt, 1:2], ALU.is_equal, ALU.mult))
        wait(dve, done)
        st.comb_ready = c_dve.after(dve.tensor_tensor(st.comb[:, :, 0:E0], st.comb[:, :, 0:E0], st.pick[:],
                                                      ALU.add))

    def load_expert(st, layer):
        slot, weights, free = experts.take()
        wait(sp, free)
        loaded = c_expert[slot].after(sp.dma_start(
            weights[:].rearrange("p a n -> p (a n)"), t["experts"][layer * E0 + st.loads]))
        st.loaded.append((slot, weights, loaded))
        st.loads += 1

    def experts_of(st, layer, residual_ready):
        count = E0 if layer == 0 else E1 + 1
        if layer == 0:
            yield at(st.comb_ready, small.next())
            slot, ps, free = small.take()
            wait(pe, st.comb_ready, free)
            for qt in range(QT):
                last = pe.transpose(ps[0:E0, qt * P:(qt + 1) * P], st.comb[:, qt, 0:E0], ident[:])
            st.comb_read = turned = c_pe.after(last)
            wait(act, turned, st.tmpT_read)
            copied = c_act.after(act.activation(st.tmpT[0:E0, :], ps[0:E0, 0:S], ACT.Copy))
            small.release(slot, copied)
            yield at(copied, small.next())
            slot, ps, free = small.take()
            wait(pe, copied, free)
            for qt in range(QT):
                last = pe.matmul(ps[:, qt * D:(qt + 1) * D], st.tmpT[0:E0, qt * P:(qt + 1) * P], b_eo[:],
                                 start=True, stop=True)
            st.tmpT_read = made = c_pe.after(last)
            wait(dve, made, residual_ready)
            flat = st.x[:].rearrange("p a d -> p (a d)")
            residual_ready = c_dve.after(dve.tensor_tensor(flat, ps[:, 0:QT * D], flat, ALU.add))
            small.release(slot, residual_ready)
        def first(e):
            eslot, weights, loaded = st.loaded.pop(0)
            slot, ps, free = scores.take()
            wait(pe, loaded, st.xT_ready, free)
            for f in range(NF):
                last = pe.matmul(ps[:, f, :], weights[:, 0, f * P:(f + 1) * P], st.xT[:], start=True, stop=True)
            st.xT_read = made = c_pe.after(last, 0.95)
            hslot, hid, hfree = hidden.take()
            wait(act, made, hfree)
            if layer == 0:
                for f in range(NF):
                    ready = c_act.after(act.activation(hid[:, f, :], ps[:, f, :], ACT.Gelu,
                                                       bias=b_hid[:, e, f:f + 1]), 0.42)
            else:
                ready = c_act.after(act.activation(hid[:], ps[:], ACT.Tanh, scale=0.5), 0.9)
                wait(dve, ready)
                ready = c_dve.after(dve.scalar_tensor_tensor(
                    out=hid[:].rearrange("p a b -> p (a b)"), in0=hid[:].rearrange("p a b -> p (a b)"), scalar=1.0,
                    in1=ps[:].rearrange("p a b -> p (a b)"), op0=ALU.add, op1=ALU.mult), 1.14)
            scores.release(slot, ready)
            return e, eslot, weights, hslot, hid, ready

        def second(e, eslot, weights, hslot, hid, ready):
            slot, ps, free = small.take()
            wait(pe, ready, free)
            for qt in range(QT):
                for f in range(NF):
                    last = pe.matmul(ps[:, qt * D:(qt + 1) * D], hid[:, f, qt * P:(qt + 1) * P],
                                     weights[:, 1, f * D:(f + 1) * D], start=f == 0, stop=f == NF - 1)
            made = c_pe.after(last, 0.87)
            hidden.release(hslot, made)
            experts.release(eslot, made)
            wait(dve, made, st.x_ready, residual_ready, st.comb_ready)
            for qt in range(QT):
                st.x_ready = c_dve.after(dve.scalar_tensor_tensor(
                    out=st.x[:, qt, :], in0=ps[:, qt * D:(qt + 1) * D], scalar=st.comb[:, qt, e:e + 1],
                    in1=st.x[:, qt, :], op0=ALU.mult, op1=ALU.add), 0.26)
            small.release(slot, st.x_ready)

        before = None
        for e in range(count):
            if not st.loaded:
                if before is not None:
                    yield at(before[-1], small.next()) + LAG["second"]
                    second(*before)
                    before = None
                yield from until_free(experts)
                load_expert(st, layer)
            if st.loads < count and experts.free:
                load_expert(st, layer)
            if not hidden.free and before is not None:
                yield at(before[-1], small.next()) + LAG["second"]
                second(*before)
                before = None
            yield from until_free(hidden)
            yield at(st.loaded[0][2], st.xT_ready, scores.next()) + LAG["first"]
            if not hidden.free:
                yield from until_free(hidden)
            begun = first(e)
            if before is not None:
                yield at(before[-1], small.next()) + LAG["second"]
                second(*before)
            before = begun
        yield at(before[-1], small.next()) + LAG["second"]
        second(*before)
        st.comb_read = st.x_ready
        st.loads = 0

    def load_x(st, batch):
        wait(sp, st.x_in_read)
        st.x_loaded = st.c_x.after(sp.dma_start(
            st.x_in[:], t["x"][bass.ds(batch, 1)].rearrange("a (q p) d -> (a p) q d", p=P)))

    def first_layer(st, batch, prepare_context):
        yield from transpose_state(st, st.x_in, st.x_loaded)
        steps = [self_attention(st, 0, causal_q, causal_k, None, 0, st.x_loaded, st.x_in)]
        if prepare_context:
            steps.append(context(st, 0, batch))
        yield from alternate(*steps)
        yield from layer_norm(st, st.x_ready, 2, 3)
        yield from transpose_state(st, st.x, st.x_ready)
        yield from cross_attention(st, 0, None, None, None, 1, st.xT_ready)
        yield from layer_norm(st, st.x_ready, 4, 5)
        yield from transpose_state(st, st.x, st.x_ready)
        yield from route(st, 0, st.x_ready)
        yield from alternate(experts_of(st, 0, st.x_ready), context(st, 1, batch), masks(st, batch))

    def second_layer(st, batch, next_batch):
        yield from layer_norm(st, st.x_ready, 6, 7)
        yield from rms_norm(st, st.x_ready, 8)
        yield from transpose_state(st, st.tmp, st.normed)
        yield from self_attention(st, 1, st.mself_q, st.mself_k, st.mself_ready, None, st.normed, st.x)
        yield from rms_norm(st, st.x_ready, 9)
        yield from transpose_state(st, st.tmp, st.normed)
        yield from cross_attention(st, 1, mask_bias_q, mask_bias_k, st.mcross_ready, None, st.normed)
        cross_bias.release(0, st.keys_read)
        yield from rms_norm(st, st.x_ready, 10)
        yield from transpose_state(st, st.tmp, st.normed)
        yield from route(st, 1, st.normed)
        wait(dve, st.comb_read)
        st.comb_ready = c_dve.after(dve.memset(st.comb[:, :, E1:E1 + 1], 0.5))
        steps = [experts_of(st, 1, st.x_ready)]
        if next_batch is not None:
            load_x(st, next_batch)
            steps.append(context(st, 0, next_batch))
        yield from alternate(*steps)
        yield at(st.x_ready)
        wait(sp, st.x_ready)
        st.stored = st.c_out.after(sp.dma_start(
            out[bass.ds(batch, 1)].rearrange("a (q p) d -> (a p) q d", p=P), st.x[:]))
        if next_batch is None:
            wait(sp, st.stored)

    def issue(*steps):
        for _ in alternate(*steps):
            pass

    odd, even = streams
    load_x(even, 0)
    load_x(odd, 1)
    issue(first_layer(even, 0, True), context(odd, 0, 1))
    restart()
    with nc.Fori(0, PAIRS - 1) as i:
        issue(later(LAG["odd"], first_layer(odd, i * 2 + 1, False), second_layer(odd, i * 2 + 1, i * 2 + 3)),
              chain(second_layer(even, i * 2, i * 2 + 2), first_layer(even, i * 2 + 2, False)))
        restart()
    issue(chain(first_layer(odd, B - 1, False), second_layer(odd, B - 1, None)), second_layer(even, B - 2, None))


def kernel(**inputs):
    import concourse.bacc as bacc
    from concourse.bass_utils import run_bass_kernel_spmd

    a = {k: np.asarray(v) for k, v in inputs.items()}
    f32 = np.float32

    def layer(n):
        return lambda name: a[f"L{n}_xattn_{name}"]

    l0, l1 = layer(0), layer(1)
    zero = np.zeros(D, f32)

    def values(w):
        padded = np.zeros((D, H, VW), f32)
        padded[:, :, :HD] = w.reshape(D, H, HD)
        return padded.reshape(D, VCOLS)

    def value_bias(b):
        padded = np.ones((H, VW), f32)
        padded[:, :HD] = b.reshape(H, HD)
        return np.broadcast_to(padded.reshape(1, VCOLS), (P, VCOLS))

    def thrice(w):
        return np.repeat(w.reshape(D, NG, 1, GR), 3, axis=2).reshape(D, NG, QROWS)

    def row_bias(b):
        return np.tile(b.reshape(NG, GR).T, (3, 1))

    tri = np.tril(np.ones((S, S), bool))
    causal = np.where(tri, f32(0), f32(-BIG)).astype(f32)

    def tiles(m):
        return m.reshape(QT, P, S).transpose(1, 0, 2)

    def expert(w1, w2):
        return np.concatenate([w1, w2.reshape(NF, P, D).transpose(1, 0, 2).reshape(P, NF * D)], axis=1)

    w1s = [l0("e_w1")[e] for e in range(E0)] + [l1("exp_w1")[e].T for e in range(E1)] + [l1("sh_w1").T]
    w2s = [l0("e_w2")[e] for e in range(E0)] + [l1("exp_w2")[e].T for e in range(E1)] + [l1("sh_w2").T]
    arrays = {
        "x": a["x"],
        "ctxT": a["ctx_1024"].transpose(0, 2, 1),
        "mself": a["mask_BxSxS_ik0"],
        "mselfT": a["mask_BxSxS_ik0"].transpose(0, 2, 1),
        "mcross": a["mask_BxSxS2_if1"],
        "mcrossT": a["mask_BxSxS2_if1"].transpose(0, 2, 1),
        "ident": np.eye(P, dtype=f32),
        "head_sel": np.tile(np.kron(np.eye(HG, dtype=f32), np.ones((HD, 1), f32)), (3, 1)),
        "iota": np.broadcast_to(np.arange(E0, dtype=f32), (P, E0)),
        "causal_q": tiles(causal),
        "causal_k": tiles(causal.T),
        "w_split": np.stack([
            np.stack([thrice(l0("sa_wq")), thrice(l0("sa_wk")), thrice(l0("ca_wq"))]),
            np.stack([thrice(l1("sa_wq").T), thrice(l1("sa_wk").T), thrice(l1("ca_wq").T)]),
        ]).transpose(2, 0, 1, 3, 4),
        "w_key": np.stack([l0("ca_wk"), l1("ca_wk").T], axis=1),
        "w_val": np.stack([np.stack([values(l0("sa_wv")), values(l0("ca_wv"))]),
                           np.stack([values(l1("sa_wv").T), values(l1("ca_wv").T)])]).transpose(2, 0, 1, 3),
        "w_out": np.stack([np.stack([l0("sa_wo"), l0("ca_wo")]),
                           np.stack([l1("sa_wo").T, l1("ca_wo").T])]).transpose(2, 0, 1, 3),
        "b_q": np.stack([np.stack([row_bias(l0("sa_bq")), row_bias(l0("sa_bk")), row_bias(l0("ca_bq"))]),
                         np.stack([row_bias(zero)] * 3)]).transpose(2, 0, 1, 3),
        "b_k": np.stack([l0("ca_bk"), zero], axis=1),
        "b_val": np.stack([np.stack([value_bias(l0("sa_bv")), value_bias(l0("ca_bv"))]),
                           np.stack([value_bias(zero)] * 2)]).transpose(2, 0, 1, 3),
        "rows": np.broadcast_to(np.stack([
            l0("sa_bo"), l0("ca_bo"), l0("ln1_g"), l0("ln1_b"), l0("ln2_g"), l0("ln2_b"), l0("ln3_g"),
            l0("ln3_b"), l1("norm1_w"), l1("norm2_w"), l1("norm3_w")]), (P, 11, D)),
        "router": np.stack([l0("router_w"), l1("gate_w").T], axis=1),
        "router_b": np.broadcast_to(l0("router_b"), (P, E0)),
        "b_hid": l0("e_b1").reshape(E0, NF, P).transpose(2, 0, 1),
        "b_eo": l0("e_b2"),
        "halves": np.full((P, 2), -0.5, f32),
        "experts": np.stack([expert(w1, w2) for w1, w2 in zip(w1s, w2s)]),
    }
    arrays = {k: np.ascontiguousarray(v) for k, v in arrays.items()}
    nc = bacc.Bacc("TRN2", target_bir_lowering=False, num_devices=1, dynamic_dma_scratch_size=1024)
    t = {k: nc.dram_tensor(f"in_{k}", v.shape, mybir.dt.from_np(v.dtype), kind="ExternalInput").ap()
         for k, v in arrays.items()}
    out = nc.dram_tensor("out_x", (B, S, D), F32, kind="ExternalOutput").ap()
    build(nc, t, out)
    r = run_bass_kernel_spmd(nc, [{f"in_{k}": v for k, v in arrays.items()}], core_ids=[0])
    return r.results[0]["out_x"]
```
